# Optimizing a Trainium2 kernel written in Bass

```python
import numpy as np
import jax
import jax.numpy as jnp

def _softmax(x, axis=-1):
    return jax.nn.softmax(x, axis=axis)

def _gelu(x):
    return jax.nn.gelu(x, approximate=True)

def _silu(x):
    return jax.nn.silu(x)

def _sigmoid(x):
    return jax.nn.sigmoid(x)

def _layernorm(x, axis=-1, eps=1e-05):
    m = jnp.mean(x, axis=axis, keepdims=True)
    v = jnp.var(x, axis=axis, keepdims=True)
    return (x - m) / jnp.sqrt(v + eps)

def _scatter_add(tgt, idx, src, axis=0):
    return tgt.at[idx].add(src)

def _segment_sum(src, seg, n):
    return jax.ops.segment_sum(src, seg, n)
kernel_name = 'mk_lm_tower_d1_tok_ids256_r4_776bfb'

def setup_inputs(seed: int=0):
    np.random.seed(seed)
    _w = jnp.asarray

    def _rec_inputs():
        import jax
        import jax.numpy as jnp
        _rk = jax.random.key(seed)
        x = jax.random.randint(jax.random.fold_in(_rk, 1), (2, 2048), 0, 128, jnp.int32)
        return x
    x = _rec_inputs()

    def _L0_tok_setup():
        import jax, jax.numpy as jnp
        import numpy as np
        VOCAB = 128
        D = 64
        S = 128
        B = 128
        MAX_LEN = 128
        SEP_ID = 13
        PAD_ID = 1

        def _make_pe():
            pos = np.arange(MAX_LEN, dtype=np.float32)[:, None]
            div = np.exp(np.arange(0, D, 2, dtype=np.float32) * (-np.log(10000.0) / D))
            pe = np.zeros((MAX_LEN, D), dtype=np.float32)
            pe[:, 0::2] = np.sin(pos * div)
            pe[:, 1::2] = np.cos(pos * div)
            return jnp.asarray(pe)
        key = jax.random.key(seed)
        k1, k2 = jax.random.split(key)
        sequence = jax.random.randint(k1, (S, B), 0, VOCAB)
        token_W = jax.random.normal(k2, (VOCAB, D), dtype=jnp.float32) * 0.02
        token_W = token_W.at[0].set(0.0)
        pe = _make_pe()
        return {'sequence': sequence, 'token_W': token_W, 'pe': pe}
    _L0_tok_all = _L0_tok_setup()
    _L0_tok_in = {k: v for k, v in _L0_tok_all.items() if k in ('token_W', 'pe')}
    del _L0_tok_all

    def _L0_attn_setup():
        import jax, jax.numpy as jnp
        import numpy as np
        SEQ_LEN = 512
        EMBED_DIM = 64
        BATCH = 8
        LN_EPS = 1e-05

        def _layernorm(x, g, b):
            mu = jnp.mean(x, axis=-1, keepdims=True)
            var = jnp.mean(jnp.square(x - mu), axis=-1, keepdims=True)
            return (x - mu) * jax.lax.rsqrt(var + LN_EPS) * g + b
        key = jax.random.key(seed)
        ks = jax.random.split(key, 8)
        C = EMBED_DIM
        x = jax.random.normal(ks[0], (BATCH, SEQ_LEN, C), dtype=jnp.float32)
        qkv_w = jax.random.normal(ks[1], (C, 3 * C), dtype=jnp.float32) * 0.02
        qkv_b = jnp.zeros((3 * C,), dtype=jnp.float32)
        proj_w = jax.random.normal(ks[2], (C, C), dtype=jnp.float32) * 0.02
        proj_b = jnp.zeros((C,), dtype=jnp.float32)
        ln1_g = jnp.ones((C,), dtype=jnp.float32)
        ln1_b = jnp.zeros((C,), dtype=jnp.float32)
        ln2_g = jnp.ones((C,), dtype=jnp.float32)
        ln2_b = jnp.zeros((C,), dtype=jnp.float32)
        bias_table = jax.random.truncated_normal(ks[3], -2.0, 2.0, (2 * SEQ_LEN - 1,), dtype=jnp.float32) * 0.02
        scale = jnp.asarray(1.0 / np.sqrt(C), dtype=jnp.float32)
        return {'x': x, 'ln1_g': ln1_g, 'ln1_b': ln1_b, 'qkv_w': qkv_w, 'qkv_b': qkv_b, 'bias_table': bias_table, 'scale': scale, 'proj_w': proj_w, 'proj_b': proj_b, 'ln2_g': ln2_g, 'ln2_b': ln2_b}
    _L0_attn_all = _L0_attn_setup()
    _L0_attn_in = {k: v for k, v in _L0_attn_all.items() if k in ('ln1_g', 'ln1_b', 'qkv_w', 'qkv_b', 'bias_table', 'scale', 'proj_w', 'proj_b', 'ln2_g', 'ln2_b')}
    del _L0_attn_all

    def _L0_ffn_setup():
        import jax, jax.numpy as jnp
        import numpy as np
        D_MODEL = 64
        EXPERT_DIM = 128
        NUM_EXPERTS = 8
        TOP_K = 2
        SEQ_LEN = 512
        BATCH = 2
        key = jax.random.key(seed)
        ks = jax.random.split(key, 8)
        s = 0.02
        x = jax.random.normal(ks[0], (SEQ_LEN, BATCH, D_MODEL), dtype=jnp.float32)
        Wg = jax.random.normal(ks[1], (D_MODEL, NUM_EXPERTS), dtype=jnp.float32) * s
        bg = jax.random.normal(ks[2], (NUM_EXPERTS,), dtype=jnp.float32) * s
        bias = jnp.zeros((NUM_EXPERTS,), dtype=jnp.float32)
        W1 = jax.random.normal(ks[3], (NUM_EXPERTS, D_MODEL, EXPERT_DIM), dtype=jnp.float32) * s
        b1 = jax.random.normal(ks[4], (NUM_EXPERTS, EXPERT_DIM), dtype=jnp.float32) * s
        W2 = jax.random.normal(ks[5], (NUM_EXPERTS, EXPERT_DIM, D_MODEL), dtype=jnp.float32) * s
        b2 = jax.random.normal(ks[6], (NUM_EXPERTS, D_MODEL), dtype=jnp.float32) * s
        return {'x': x, 'Wg': Wg, 'bg': bg, 'bias': bias, 'W1': W1, 'b1': b1, 'W2': W2, 'b2': b2}
    _L0_ffn_all = _L0_ffn_setup()
    _L0_ffn_in = {k: v for k, v in _L0_ffn_all.items() if k in ('Wg', 'bg', 'bias', 'W1', 'b1', 'W2', 'b2')}
    del _L0_ffn_all
    return {'x': x, 'L0_tok_token_W': _L0_tok_in['token_W'], 'L0_tok_pe': _L0_tok_in['pe'], 'L0_attn_ln1_g': _L0_attn_in['ln1_g'], 'L0_attn_ln1_b': _L0_attn_in['ln1_b'], 'L0_attn_qkv_w': _L0_attn_in['qkv_w'], 'L0_attn_qkv_b': _L0_attn_in['qkv_b'], 'L0_attn_bias_table': _L0_attn_in['bias_table'], 'L0_attn_scale': _L0_attn_in['scale'], 'L0_attn_proj_w': _L0_attn_in['proj_w'], 'L0_attn_proj_b': _L0_attn_in['proj_b'], 'L0_attn_ln2_g': _L0_attn_in['ln2_g'], 'L0_attn_ln2_b': _L0_attn_in['ln2_b'], 'L0_ffn_Wg': _L0_ffn_in['Wg'], 'L0_ffn_bg': _L0_ffn_in['bg'], 'L0_ffn_bias': _L0_ffn_in['bias'], 'L0_ffn_W1': _L0_ffn_in['W1'], 'L0_ffn_b1': _L0_ffn_in['b1'], 'L0_ffn_W2': _L0_ffn_in['W2'], 'L0_ffn_b2': _L0_ffn_in['b2']}

def reference(x, L0_tok_token_W, L0_tok_pe, L0_attn_ln1_g, L0_attn_ln1_b, L0_attn_qkv_w, L0_attn_qkv_b, L0_attn_bias_table, L0_attn_scale, L0_attn_proj_w, L0_attn_proj_b, L0_attn_ln2_g, L0_attn_ln2_b, L0_ffn_Wg, L0_ffn_bg, L0_ffn_bias, L0_ffn_W1, L0_ffn_b1, L0_ffn_W2, L0_ffn_b2):
    import jax
    import jax.numpy as jnp

    def _L0_tok_ref(sequence, token_W, pe):
        import jax, jax.numpy as jnp
        import numpy as np
        VOCAB = 128
        D = 64
        S = 128
        B = 128
        MAX_LEN = 128
        SEP_ID = 13
        PAD_ID = 1

        def _make_pe():
            pos = np.arange(MAX_LEN, dtype=np.float32)[:, None]
            div = np.exp(np.arange(0, D, 2, dtype=np.float32) * (-np.log(10000.0) / D))
            pe = np.zeros((MAX_LEN, D), dtype=np.float32)
            pe[:, 0::2] = np.sin(pos * div)
            pe[:, 1::2] = np.cos(pos * div)
            return jnp.asarray(pe)
        tok_emb = token_W[sequence] * (sequence != 0)[..., None].astype(token_W.dtype)
        S_, B_ = sequence.shape

        def step(carry, xs):
            prev_sep, pad_num = carry
            tok, j = xs
            is_sep = tok == SEP_ID
            skip = prev_sep & (tok == PAD_ID) & ~is_sep
            pos_emb = pe[j - pad_num]
            emb = jnp.where(skip[:, None], jnp.zeros((), pe.dtype), pos_emb)
            new_carry = (is_sep | skip, pad_num + skip.astype(pad_num.dtype))
            return (new_carry, emb)
        init = (jnp.zeros((B_,), dtype=bool), jnp.zeros((B_,), dtype=jnp.int32))
        _, pos_emb = jax.lax.scan(step, init, (sequence, jnp.arange(S_, dtype=jnp.int32)))
        return tok_emb + pos_emb

    def _L0_attn_ref(x, ln1_g, ln1_b, qkv_w, qkv_b, bias_table, scale, proj_w, proj_b, ln2_g, ln2_b):
        import jax, jax.numpy as jnp
        import numpy as np
        SEQ_LEN = 512
        EMBED_DIM = 64
        BATCH = 8
        LN_EPS = 1e-05

        def _layernorm(x, g, b):
            mu = jnp.mean(x, axis=-1, keepdims=True)
            var = jnp.mean(jnp.square(x - mu), axis=-1, keepdims=True)
            return (x - mu) * jax.lax.rsqrt(var + LN_EPS) * g + b
        B, N, C = x.shape
        h = _layernorm(x, ln1_g, ln1_b)
        qkv = h @ qkv_w + qkv_b
        q, k, v = jnp.split(qkv, 3, axis=-1)
        coords = jnp.arange(N)
        rel_idx = coords[None, :] - coords[:, None] + (N - 1)
        rel_bias = bias_table[rel_idx]
        attn = jnp.einsum('bnc,bmc->bnm', q, k) + rel_bias
        attn = jax.nn.softmax(attn, axis=-1) * scale
        out = jnp.einsum('bnm,bmc->bnc', attn, v)
        out = out @ proj_w + proj_b
        out = _layernorm(out, ln2_g, ln2_b)
        return out

    def _L0_ffn_ref(x, Wg, bg, bias, W1, b1, W2, b2):
        import jax, jax.numpy as jnp
        import numpy as np
        D_MODEL = 64
        EXPERT_DIM = 128
        NUM_EXPERTS = 8
        TOP_K = 2
        SEQ_LEN = 512
        BATCH = 2
        x_flat = x.reshape(-1, D_MODEL)
        gate_logits = x_flat @ Wg + bg + bias
        topk_vals, topk_idx = jax.lax.top_k(gate_logits, TOP_K)
        topk_w = jax.nn.softmax(topk_vals, axis=-1)
        combine = (jax.nn.one_hot(topk_idx, NUM_EXPERTS, dtype=x.dtype) * topk_w[..., None]).sum(axis=1)
        h = jax.nn.relu(jnp.einsum('td,edh->teh', x_flat, W1) + b1)
        y = jnp.einsum('teh,ehd->ted', h, W2) + b2
        out = jnp.einsum('ted,te->td', y, combine)
        return out.reshape(x.shape)
    h = _L0_tok_ref(x, L0_tok_token_W, L0_tok_pe)
    h = h + _L0_attn_ref(_layernorm(h, axis=-1), L0_attn_ln1_g, L0_attn_ln1_b, L0_attn_qkv_w, L0_attn_qkv_b, L0_attn_bias_table, L0_attn_scale, L0_attn_proj_w, L0_attn_proj_b, L0_attn_ln2_g, L0_attn_ln2_b)
    h = h + _L0_ffn_ref(_layernorm(h, axis=-1), L0_ffn_Wg, L0_ffn_bg, L0_ffn_bias, L0_ffn_W1, L0_ffn_b1, L0_ffn_W2, L0_ffn_b2)
    return h

_drawn_inputs = setup_inputs


def setup_inputs(seed=0):
    import zlib

    import numpy as np

    out = dict(_drawn_inputs(seed))
    spreads = {'L0_attn_ln1_g': (1.0, 0.6),
     'L0_attn_ln1_b': (0.0, 2.0),
     'L0_attn_qkv_b': (0.0, 0.493),
     'L0_attn_proj_b': (0.0, 0.1),
     'L0_attn_ln2_g': (1.0, 0.2),
     'L0_attn_ln2_b': (0.0, 0.1),
     'L0_ffn_bias': (0.0, 0.344)}
    factors = {'L0_tok_token_W': 3.851,
     'L0_attn_bias_table': 64.0,
     'L0_ffn_Wg': 8.0,
     'L0_ffn_bg': 12.755,
     'L0_ffn_W1': 4.897,
     'L0_ffn_b1': 8.0,
     'L0_ffn_W2': 3.584,
     'L0_ffn_b2': 6.142}
    for name, (base, spread) in spreads.items():
        noise = np.random.default_rng([zlib.crc32(name.encode()), seed]).standard_normal(out[name].shape)
        drawn = base * np.exp(spread * noise) if base else spread * noise
        out[name] = jnp.asarray(drawn.astype(out[name].dtype))
    for name, factor in factors.items():
        out[name] = (out[name] * factor).astype(out[name].dtype)
    return out
```

```python
from contextlib import ExitStack

import concourse.bass as bass
from concourse import mybir

F32 = mybir.dt.float32
F16 = mybir.dt.float16
BF16 = mybir.dt.bfloat16
I32 = mybir.dt.int32
U32 = mybir.dt.uint32
ALU = mybir.AluOpType
ACT = mybir.ActivationFunctionType
AX = mybir.AxisListType

P = 128
VOCAB = 128
D = 64
SEQS, LEN = 2, 2048
ROWS = LEN // P
TABLE = 1023
FIRST = LEN // 2
SEP_ID, PAD_ID = 13, 1
SKIP_ID = 128
EXPERTS, HID = 8, 128
EPS = 1e-5
ABSENT = -1e30
ESCALE = 32768.0
XSCALE = 64.0
TOE = 1408
TOE_FLAT = TOE - 1024
NQ = 4
BLOCKS = 18
TRIO = 3
TRIOS = BLOCKS // TRIO
HALF = 512
S0, S1, SK = 0, 128, 257
GW = 386


def build(nc, x, token_w, pe, ln1_g, ln1_b, qkv_w, qkv_b, bias_table, scale, proj_w, proj_b, ln2_g, ln2_b,
          gate_w, gate_b, gate_bias, w1, b1, w2, b2, out):
    ids_dram = nc.dram_tensor("ids_scratch", (SEQS, LEN), BF16, kind="Internal").ap()
    tail_dram = nc.dram_tensor("tail_scratch", (1, 256), F32, kind="Internal").ap()

    with ExitStack() as ctx:
        def sb(name, shape, dt=F32):
            return ctx.enter_context(nc.sbuf_tensor(name, shape, dt))

        def sem(name):
            return ctx.enter_context(nc.semaphore(name))

        bank = [ctx.enter_context(nc.psum_tensor(f"bank{i}", [P, 512], F32)) for i in range(8)]

        iota_row = sb("iota_row", [P, P])
        iota_h = sb("iota_h", [P, P], F16)
        iota_p = sb("iota_p", [P, 1])
        ident = sb("ident", [P, P])
        ident_h = sb("ident_h", [P, P], F16)
        ident_b = sb("ident_b", [P, P], BF16)
        ones_h = sb("ones_h", [P, P], F16)
        ones_b = sb("ones_b", [P, P], BF16)
        neghalf = sb("neghalf", [P, 8])
        ids_i = sb("ids_i", [ROWS, SEQS, P], I32)
        ids_f = sb("ids_f", [ROWS, SEQS, P])
        is_sep = sb("is_sep", [ROWS, P])
        is_pad = sb("is_pad", [ROWS, P])
        ids_b = sb("ids_b", [ROWS, SEQS, P], BF16)
        id_col = sb("id_col", [P, SEQS * ROWS])
        oneh_j = sb("oneh_j", [P, SEQS * ROWS, P], F16)
        skip_j = sb("skip_j", [P, ROWS], F16)
        ids_all = sb("ids_all", [P, SEQS * LEN + 1], BF16)
        oneh_t = sb("oneh_t", [P, SEQS * LEN + 1], F16)
        skip_row = sb("skip_row", [1, LEN + 1], F16)
        table_all = sb("table_all", [P, TABLE])
        hankel = sb("hankel", [P, 1024])
        nbmax = sb("nbmax", [P, 1])
        toe_hi = sb("toe_hi", [P, TOE], F16)
        toe_lo = sb("toe_lo", [P, TOE], F16)
        flat = sb("flat", [P, 1])
        w_tok = sb("w_tok", [P, D])
        pe_all = sb("pe_all", [P, SEQS, D])
        g1_all = sb("g1_all", [P, D])
        b1_all = sb("b1_all", [P, D])
        g2_all = sb("g2_all", [P, D])
        b2_all = sb("b2_all", [P, D])
        pb_all = sb("pb_all", [P, D])
        sc_all = sb("sc_all", [P, 1])
        qkv_sb = sb("qkv_sb", [D + 1, 3 * D])
        proj_sb = sb("proj_sb", [D, D])
        gate_sb = sb("gate_sb", [P, EXPERTS])
        gate_hi = sb("gate_hi", [P, EXPERTS], F16)
        gate_lo = sb("gate_lo", [P, EXPERTS], F16)
        gb_all = sb("gb_all", [P, 2, EXPERTS])
        gb_sum = sb("gb_sum", [P, EXPERTS])
        w1_sb = sb("w1_sb", [P, EXPERTS, HID])
        w1_hi = sb("w1_hi", [P, EXPERTS, HID], F16)
        w1_lo = sb("w1_lo", [P, EXPERTS, HID], F16)
        w2_sb = sb("w2_sb", [P, EXPERTS, D])
        eb1_sb = sb("eb1_sb", [EXPERTS, HID])
        eb1_col = sb("eb1_col", [P, EXPERTS])
        eb2_sb = sb("eb2_sb", [EXPERTS, D])
        pmask = sb("pmask", [P, 1])
        hv = sb("hv", [P, 3, D])
        hv_part = sb("hv_part", [P, 3, 3, D], BF16)
        hv_rest = sb("hv_rest", [P, 3, D])
        vy = sb("vy", [P, 3, D])
        vstat = sb("vstat", [P, 3, 6])
        vmv = sb("vmv", [P, 3, 2])
        vvar = sb("vvar", [P, 3])
        vrs = sb("vrs", [P, 3])
        hvT = sb("hvT", [D + 1, 3 * P])
        qT = sb("qT", [D, 3 * P])
        kT = sb("kT", [D, 3 * P])
        vT = sb("vT", [D, 3 * P])
        vp = sb("vp", [P, 3, D + 1])
        vh = sb("vh", [P, SEQS, D + 1])
        vh_skip = sb("vh_skip", [1, D + 1])
        v_sel = sb("v_sel", [EXPERTS, 8, D + 1])
        cnt = sb("cnt", [P, SEQS, 3])
        cnt_half = sb("cnt_half", [P, SEQS, 3])
        skc = sb("skc", [P, ROWS])
        sk_half = sb("sk_half", [P, 3])
        flat_w = sb("flat_w", [P, SEQS, 2])
        sk_flat = sb("sk_flat", [P, 2])
        absent = sb("absent", [P, 3])
        absent_d = sb("absent_d", [P, 257], BF16)
        gmax = sb("gmax", [P, 3])
        eg = sb("eg", [P, GW])
        eg_hi = sb("eg_hi", [P, GW], F16)
        eg_lo = sb("eg_lo", [P, GW], F16)
        egT = sb("egT", [P, 3, P])
        a_sb = sb("a_sb", [P, 2, HALF])
        pT = sb("pT", [P, 4, HALF])
        sk_a = sb("sk_a", [P, 8])
        sk_p = sb("sk_p", [P, 8])
        sk_pT = sb("sk_pT", [8, P])
        u_all = sb("u_all", [P, BLOCKS, D + 1])
        h_all = sb("h_all", [P, BLOCKS, D])
        fin_all = sb("fin_all", [P, BLOCKS, D])
        o = sb("o", [P, TRIO, D])
        rden = sb("rden", [P, TRIO])
        stat = sb("stat", [P, TRIO, 6])
        mv = sb("mv", [P, TRIO, 2])
        var1 = sb("var1", [P, TRIO])
        rs1 = sb("rs1", [P, TRIO])
        var2 = sb("var2", [P, TRIO])
        rs2 = sb("rs2", [P, TRIO])
        og = sb("og", [P, TRIO, D])
        xn = sb("xn", [P, TRIO, D])
        xs = sb("xs", [P, TRIO, 2, D], F16)
        xT = sb("xT", [P, TRIO * P], F16)
        lg = sb("lg", [P, TRIO, EXPERTS])
        top = sb("top", [P, TRIO, 8])
        tix = sb("tix", [P, TRIO, 8], U32)
        tixf = sb("tixf", [P, TRIO, 2])
        gd = sb("gd", [P, TRIO])
        ge = sb("ge", [P, TRIO])
        gs = sb("gs", [P, TRIO])
        gw = sb("gw", [P, 2, TRIO])
        c1 = sb("c1", [P, TRIO, EXPERTS])
        c2 = sb("c2", [P, TRIO, EXPERTS])
        comb = sb("comb", [P, TRIO, EXPERTS])
        cT = sb("cT", [EXPERTS, TRIO * P])
        hid = sb("hid", [P, EXPERTS, TRIO * P])
        prod = sb("prod", [P, 2, EXPERTS, D])
        acc = sb("acc", [P, TRIO, D])
        res = sb("res", [P, TRIO, D])
        fin_part = sb("fin_part", [P, 3, 3, D], BF16)
        fin_rest = sb("fin_rest", [P, 3, D])
        looked = sb("looked", [P, SEQS, 8, D])
        looked1 = sb("looked1", [1, D])

        loads = {n: sem("ld_" + n) for n in (
            "ids", "table", "hankel", "tail", "scratch_tail", "scratch_ids", "ids_all", "w_tok", "pe", "ln1",
            "qkv", "proj", "ln2", "scale", "gate", "gate_b", "w1", "w2", "eb1", "eb2")}
        s_const = sem("s_const")
        s_dve = sem("s_dve")
        s_pool = sem("s_pool")
        s_ident = sem("s_ident")
        s_ids = sem("s_ids")
        s_idT = sem("s_idT")
        s_idcol = sem("s_idcol")
        s_onej = sem("s_onej")
        s_cnt = sem("s_cnt")
        s_cntread = sem("s_cntread")
        s_absent = sem("s_absent")
        s_onet = sem("s_onet")
        s_nbmax = sem("s_nbmax")
        s_expb = sem("s_expb")
        s_toe = sem("s_toe")
        s_vvar = sem("s_vvar")
        s_vrs = sem("s_vrs")
        s_hl = sem("s_hl")
        s_hT = sem("s_hT")
        s_hTsb = sem("s_hTsb")
        s_qkv = sem("s_qkv")
        s_qsb = sem("s_qsb")
        s_ksb = sem("s_ksb")
        s_vproj = sem("s_vproj")
        s_g = sem("s_g")
        s_gmax = sem("s_gmax")
        s_eg = sem("s_eg")
        s_egs = sem("s_egs")
        s_egT = sem("s_egT")
        s_egTsb = sem("s_egTsb")
        s_vh = sem("s_vh")
        s_hpart = sem("s_hpart")
        s_m = sem("s_m")
        s_a = sem("s_a")
        s_asb = sem("s_asb")
        s_p = sem("s_p")
        s_sk = sem("s_sk")
        s_skp = sem("s_skp")
        s_skT = sem("s_skT")
        s_skTsb = sem("s_skTsb")
        s_u = sem("s_u")
        s_usb = sem("s_usb")
        s_hsb = sem("s_hsb")
        s_eb1T = sem("s_eb1T")
        s_eb1 = sem("s_eb1")
        s_w1s = sem("s_w1s")
        s_var1 = sem("s_var1")
        s_rs1 = sem("s_rs1")
        s_on = sem("s_on")
        s_h2 = sem("s_h2")
        s_var2 = sem("s_var2")
        s_rs2 = sem("s_rs2")
        s_xs = sem("s_xs")
        s_xT = sem("s_xT")
        s_xTsb = sem("s_xTsb")
        s_lg = sem("s_lg")
        s_gd = sem("s_gd")
        s_ge = sem("s_ge")
        s_comb = sem("s_comb")
        s_z = sem("s_z")
        s_hid = sem("s_hid")
        s_cT = sem("s_cT")
        s_cTsb = sem("s_cTsb")
        s_cb = sem("s_cb")
        s_res = sem("s_res")
        s_y = sem("s_y")
        s_prod = sem("s_prod")
        s_fin = sem("s_fin")
        s_fpart = sem("s_fpart")
        s_look = sem("s_look")
        s_looked0 = sem("s_looked0")
        s_looked1 = sem("s_looked1")
        s_out = sem("s_out")

        def bcast(ap, shape, axis):
            return ap.unsqueeze(axis).to_broadcast(shape)

        def tile_s(t):
            return 1 - t // 2, t % 2

        M_BANK = [7, 0, 1, 2]
        A_BANK = [5, 6]

        class Chain:

            def __init__(self, eng, s):
                self.eng, self.s, self.base, self.n = eng, s, 0, 0

            def link(self, ins):
                self.n += 1
                ins.then_inc(self.s, 1)
                self.eng.wait_ge(self.s, self.base + self.n)

        block = ctx.enter_context(nc.Block())

        @block.sync
        def _(sp):
            sp.dma_start(ids_i[:], x.rearrange("s (r p) -> r s p", p=P)).then_inc(loads["ids"], 16)
            sp.dma_start(tail_dram[:, 0:127], bias_table[TABLE - 127:TABLE].unsqueeze(0)).then_inc(loads["scratch_tail"], 16)
            sp.dma_start(tail_dram[0, 127:255].unsqueeze(1), bias_table[TABLE - 1:TABLE].partition_broadcast(P)).then_inc(loads["scratch_tail"], 16)
            sp.dma_start(table_all[:], bias_table.partition_broadcast(P)).then_inc(loads["table"], 16)
            sp.dma_start(hankel[:, 0:896], bass.AP(bias_table.tensor, 0, [[1, P], [1, 896]])).then_inc(loads["hankel"], 16)
            sp.wait_ge(loads["scratch_tail"], 32)
            sp.dma_start(hankel[:, 896:1024], bass.AP(tail_dram.tensor, 0, [[1, P], [1, P]])).then_inc(loads["tail"], 16)
            sp.wait_ge(s_ids, 1)
            sp.dma_start(ids_dram.rearrange("s (r p) -> r s p", p=P), ids_b[:]).then_inc(loads["scratch_ids"], 16)
            sp.wait_ge(loads["scratch_ids"], 16)
            sp.dma_start(ids_all[:, 0:SEQS * LEN],
                         ids_dram.rearrange("s n -> (s n)").partition_broadcast(P)).then_inc(loads["ids_all"], 16)
            for side in range(2):
                sp.dma_start(w1_sb[side * D:(side + 1) * D, :, :], w1.rearrange("e d h -> d e h")).then_inc(loads["w1"], 16)
            sp.dma_start(w2_sb[:], w2.rearrange("e h d -> h e d")).then_inc(loads["w2"], 16)
            stores = 0
            for k in range(TRIOS):
                sp.wait_ge(s_fin, k + 1)
                for b in range(TRIO * k, TRIO * k + TRIO):
                    if b < 2:
                        continue
                    s = 1 if b < 10 else 0
                    r0 = FIRST + P * (b - 2 if s else b - 10)
                    p0 = 1 if b == 2 else 0
                    sp.dma_start(out[s, r0 + p0:r0 + P, :], fin_all[p0:P, b, :]).then_inc(s_out, 16)
                    stores += 1
            for s in range(SEQS):
                sp.wait_ge((s_looked0, s_looked1)[s], 1)
                sp.dma_start(out[s, 0:FIRST, :].rearrange("(n p) d -> p n d", p=P), looked[:, s, :, :]).then_inc(s_out, 16)
                stores += 1
            sp.wait_ge(s_looked1, 2)
            sp.dma_start(out[1, FIRST:FIRST + 1, :], looked1[:]).then_inc(s_out, 16)
            stores += 1
            sp.wait_ge(s_out, 16 * stores)

        @block.gpsimd
        def _(pool):
            pool.iota(iota_row[:], [[1, P]], base=0, channel_multiplier=0,
                      allow_small_or_imprecise_dtypes=True)
            pool.iota(iota_p[:], [[0, 1]], base=0, channel_multiplier=1,
                      allow_small_or_imprecise_dtypes=True).then_inc(s_const, 1)
            pool.memset(neghalf[:], -0.5)
            pool.memset(vp[:], 1.0)
            pool.memset(ones_h[:], 1.0)
            pool.memset(ones_b[:], 1.0).then_inc(s_const, 1)
            for n in range(2):
                pool.wait_ge(s_const, 2)
                pool.wait_ge(s_vvar, n + 1)
                pool.tensor_tensor(vrs[:], vvar[:], neghalf[:, 0:3], ALU.pow).then_inc(s_vrs, 1)
            for k in range(TRIOS):
                pool.wait_ge(s_var1, k + 1)
                pool.tensor_tensor(rs1[:], var1[:], neghalf[:, 0:TRIO], ALU.pow).then_inc(s_rs1, 1)
                hk = h_all[:, TRIO * k:TRIO * k + TRIO, :]
                pool.wait_ge(s_on, k + 1)
                pool.tensor_tensor(og[:], o[:], bcast(g2_all[:, :], [P, TRIO, D], 1), ALU.mult).then_inc(s_pool, 1)
                pool.wait_ge(s_pool, k + 1)
                pool.tensor_tensor(hk, og[:], hk, ALU.add).then_inc(s_h2, 1)
                pool.wait_ge(s_var2, k + 1)
                pool.tensor_tensor(rs2[:], var2[:], neghalf[:, 0:TRIO], ALU.pow).then_inc(s_rs2, 1)

        @block.scalar
        def _(act):
            def load(name, dst, src, **kw):
                act.dma_start(dst, src, **kw).then_inc(loads[name], 16)

            load("w_tok", w_tok[:], token_w)
            load("w_tok", hv[:, 2, :], token_w[PAD_ID, :].partition_broadcast(P))
            load("pe", pe_all[:], pe[0:SEQS, :].partition_broadcast(P))
            load("ln1", g1_all[:], ln1_g.partition_broadcast(P))
            load("ln1", b1_all[:], ln1_b.partition_broadcast(P))
            load("qkv", qkv_sb[0:D, :], qkv_w)
            load("qkv", qkv_sb[D:D + 1, :], qkv_b.unsqueeze(0))
            load("proj", proj_sb[:], proj_w)
            load("scale", sc_all[:], scale.partition_broadcast(P))
            load("ln2", g2_all[:], ln2_g.partition_broadcast(P))
            load("ln2", b2_all[:], ln2_b.partition_broadcast(P))
            load("ln2", pb_all[:], proj_b.partition_broadcast(P))
            for side in range(2):
                load("gate", gate_sb[side * D:(side + 1) * D, :], gate_w)
            load("gate_b", gb_all[:, 0, :], gate_b.partition_broadcast(P))
            load("gate_b", gb_all[:, 1, :], gate_bias.partition_broadcast(P))
            load("eb1", eb1_sb[:], b1)
            load("eb2", eb2_sb[:], b2)
            act.preload_act_table(ACT.Exp)
            act.wait_ge(loads["hankel"], 16)
            act.wait_ge(loads["tail"], 16)
            act.wait_ge(s_nbmax, 1)
            act.activation(hankel[:], hankel[:], ACT.Exp, bias=nbmax[:, 0:1]).then_inc(s_expb, 1)
            act.wait_ge(s_hT, 1)
            act.copy(hvT[0:D, :], bank[2][0:D, 0:3 * P]).then_inc(s_hTsb, 1)
            act.wait_ge(s_qkv, 1)
            act.copy(qT[:], bank[3][0:D, 0:3 * P]).then_inc(s_qsb, 1)
            act.wait_ge(s_qkv, 3)
            act.copy(vT[:], bank[5][0:D, 0:3 * P]).then_inc(s_qsb, 1)
            act.wait_ge(s_vproj, 1)
            act.wait_ge(loads["scale"], 16)
            act.activation(vp[:, :, 0:D], bank[2][:, 0:3 * D].rearrange("p (s d) -> p s d", d=D), ACT.Copy,
                           scale=sc_all[:, 0:1]).then_inc(s_qsb, 1)
            act.wait_ge(s_gmax, 1)
            for n, (a, b) in enumerate(((S0, S1), (S1, SK), (SK, GW))):
                act.activation(eg[:, a:b], bank[6][:, a:b], ACT.Exp, bias=gmax[:, n:n + 1]).then_inc(s_eg, 1)
            act.wait_ge(s_egT, 1)
            act.copy(egT[:, 0:2, :], bank[3][:, 0:2 * P].rearrange("p (s d) -> p s d", d=P))
            act.copy(egT[0:1, 2, :], bank[3][0:1, 2 * P:3 * P]).then_inc(s_egTsb, 1)
            act.wait_ge(s_eb1T, 1)
            act.copy(eb1_col[:], bank[4][:, 0:EXPERTS]).then_inc(s_eb1, 1)

            def read_u(n):
                act.wait_ge(s_u, n + 1)
                b, w = ((0, 2), (2, 4), (6, 4), (10, 4), (14, 4))[n]
                act.copy(u_all[:, b:b + w, :],
                         bank[3][:, 0:w * (D + 1)].rearrange("p (b d) -> p b d", d=D + 1)).then_inc(s_usb, 1)

            read_u(0)
            for t in range(4):
                act.wait_ge(s_a, t + 1)
                if t >= 2:
                    act.wait_ge(s_p, t - 1)
                act.copy(a_sb[:, t % 2, :], bank[A_BANK[t % 2]][:, :]).then_inc(s_asb, 1)
                if t >= 1:
                    read_u(t)
            read_u(4)
            for k in range(TRIOS):
                act.wait_ge(s_xT, k + 1)
                act.copy(xT[:], bank[3].bitcast(F16)[:, 0:TRIO * P]).then_inc(s_xTsb, 1)

                def hidden(e):
                    n = EXPERTS * k + e
                    act.wait_ge(s_z, n + 1)
                    if k >= 1:
                        act.wait_ge(s_y, TRIO * k)
                    act.activation(hid[:, e, :], bank[n % 3][:, 0:TRIO * P], ACT.Relu, bias=eb1_col[:, e:e + 1],
                                   scale=1.0 / (XSCALE * XSCALE)).then_inc(s_hid, 1)

                hidden(0)
                act.wait_ge(s_gd, k + 1)
                act.activation(ge[:], gd[:], ACT.Exp).then_inc(s_ge, 1)
                for e in range(1, EXPERTS):
                    hidden(e)
                act.wait_ge(s_cT, k + 1)
                act.copy(cT[:], bank[3][0:EXPERTS, 0:TRIO * P]).then_inc(s_cTsb, 1)
            act.wait_ge(s_look, 2)
            act.copy(looked[:, 1, :, :], bank[1][:, :].rearrange("p (n d) -> p n d", d=D)).then_inc(s_looked1, 1)
            act.wait_ge(s_look, 3)
            act.copy(looked1[:], bank[2][0:1, 0:D]).then_inc(s_looked1, 1)

        @block.vector
        def _(dve):
            ch = Chain(dve, s_dve)
            link = ch.link

            dve.memset(hvT[D:D + 1, :], 1.0)
            dve.wait_ge(s_const, 1)
            dve.tensor_scalar(ident[:], iota_row[:], iota_p[:, 0:1], None, ALU.is_equal)
            dve.tensor_scalar(ident_h[:], iota_row[:], iota_p[:, 0:1], None, ALU.is_equal)
            dve.tensor_scalar(ident_b[:], iota_row[:], iota_p[:, 0:1], None, ALU.is_equal)
            dve.tensor_copy(iota_h[:], iota_row[:])
            dve.tensor_scalar(pmask[:], iota_p[:], 1.0, None, ALU.min).then_inc(s_ident, 1)
            dve.wait_ge(loads["ids"], 16)
            link(dve.tensor_copy(ids_f[:], ids_i[:]))
            dve.tensor_scalar(is_sep[:], ids_f[:, 0, :], float(SEP_ID), float(SKIP_ID - PAD_ID), ALU.is_equal, ALU.mult)
            link(dve.tensor_scalar(is_pad[:], ids_f[:, 1, :], float(PAD_ID), None, ALU.is_equal))
            link(dve.tensor_tensor(is_pad[:], is_pad[:], is_sep[:], ALU.mult))
            dve.tensor_copy(ids_b[:, 0, :], ids_f[:, 0, :])
            dve.tensor_tensor(ids_b[:, 1, :], ids_f[:, 1, :], is_pad[:], ALU.add).then_inc(s_ids, 1)
            dve.wait_ge(s_ident, 1)
            dve.wait_ge(loads["w_tok"], 32)
            dve.wait_ge(loads["pe"], 16)
            for s in range(SEQS):
                ins = dve.scalar_tensor_tensor(hv[:, s, :], w_tok[:], pmask[:, 0:1], pe_all[:, s, :], ALU.mult, ALU.add)
            link(ins)

            def row_stats(src, stats, means, var, n, mul, signal):
                for i in range(n):
                    ins = dve.bn_stats(stats[:, i, :], src[:, i, :])
                link(ins)
                for i in range(n):
                    ins = dve.bn_aggr(means[:, i, :], stats[:, i, :])
                link(ins)
                dve.tensor_scalar(var[:], means[:, :, 1], EPS, mul, ALU.add, ALU.mult).then_inc(signal, 1)

            def normalise(dst, src, means, rs, n):
                for i in range(n):
                    ins = dve.tensor_scalar(dst[:, i, :], src[:, i, :], means[:, i, 0:1], rs[:, i:i + 1],
                                            ALU.subtract, ALU.mult)
                return ins

            row_stats(hv, vstat, vmv, vvar, 3, 1.0, s_vvar)
            dve.wait_ge(s_idT, 1)
            dve.tensor_copy(id_col[:], bank[0].bitcast(BF16)[:, 0:2 * ROWS]).then_inc(s_idcol, 1)
            dve.wait_ge(s_vrs, 1)
            link(normalise(vy, hv, vmv, vrs, 3))
            row_stats(vy, vstat, vmv, vvar, 3, 1.0, s_vvar)
            dve.wait_ge(s_idcol, 1)
            for c in range(SEQS * ROWS):
                dve.tensor_scalar(oneh_j[:, c, :], iota_h[:], id_col[:, c:c + 1], None, ALU.is_equal)
            dve.tensor_scalar(skip_j[:], id_col[:, ROWS:2 * ROWS], float(SKIP_ID), None, ALU.is_equal).then_inc(s_onej, 1)
            dve.wait_ge(s_vrs, 2)
            link(normalise(vy, vy, vmv, vrs, 3))
            dve.wait_ge(loads["ln1"], 32)
            link(dve.tensor_tensor(vy[:], vy[:], bcast(g1_all[:, :], [P, 3, D], 1), ALU.mult))
            dve.tensor_tensor(vy[:], vy[:], bcast(b1_all[:, :], [P, 3, D], 1), ALU.add).then_inc(s_hl, 1)
            dve.wait_ge(loads["table"], 16)
            link(dve.tensor_reduce(nbmax[:], table_all[:], AX.X, ALU.max))
            dve.tensor_scalar(nbmax[:], nbmax[:], -1.0, None, ALU.mult).then_inc(s_nbmax, 1)
            dve.wait_ge(s_cnt, 1)
            dve.tensor_copy(cnt[:].rearrange("p s c -> p (s c)"), bank[1][:, 0:6])
            dve.tensor_copy(skc[:], bank[1][:, 8:8 + ROWS]).then_inc(s_cntread, 1)
            dve.wait_ge(s_cntread, 1)
            dve.tensor_copy(cnt_half[:, :, 1], cnt[:, :, 2])
            dve.tensor_tensor(cnt_half[:, :, 0], cnt[:, :, 1], cnt[:, :, 2], ALU.add)
            dve.tensor_reduce(cnt_half[:, :, 2], cnt[:], AX.X, ALU.add)
            dve.tensor_reduce(sk_half[:, 0:1], skc[:, 4:ROWS], AX.X, ALU.add)
            dve.tensor_reduce(sk_half[:, 1:2], skc[:, 8:ROWS], AX.X, ALU.add)
            link(dve.tensor_reduce(sk_half[:, 2:3], skc[:], AX.X, ALU.add))
            dve.tensor_scalar(absent[:, 0:2], cnt_half[:, :, 2], 0.0, ABSENT, ALU.is_equal, ALU.mult)
            link(dve.tensor_scalar(absent[:, 2:3], sk_half[:, 2:3], 0.0, ABSENT, ALU.is_equal, ALU.mult))
            dve.tensor_scalar(absent_d[:, 0:P], ident[:], absent[:, 0:1], None, ALU.mult)
            dve.tensor_scalar(absent_d[:, P:2 * P], ident[:], absent[:, 1:2], None, ALU.mult)
            dve.tensor_scalar(absent_d[:, 2 * P:2 * P + 1], ident[:, 0:1], absent[:, 2:3], None, ALU.mult).then_inc(s_absent, 1)
            dve.wait_ge(s_qkv, 2)
            dve.tensor_copy(kT[:], bank[4][0:D, 0:3 * P]).then_inc(s_ksb, 1)
            dve.wait_ge(s_g, 1)
            for n, (a, b) in enumerate(((S0, S1), (S1, SK), (SK, GW))):
                ins = dve.tensor_reduce(gmax[:, n:n + 1], bank[6][:, a:b], AX.X, ALU.max)
            link(ins)
            dve.tensor_scalar(gmax[:], gmax[:], -1.0, None, ALU.mult).then_inc(s_gmax, 1)
            dve.wait_ge(s_expb, 1)
            link(dve.tensor_scalar(toe_hi[:, TOE_FLAT:TOE], hankel[:, ::-1], ESCALE, None, ALU.mult))
            link(dve.scalar_tensor_tensor(toe_lo[:, TOE_FLAT:TOE], hankel[:, ::-1], ESCALE, toe_hi[:, TOE_FLAT:TOE],
                                          ALU.mult, ALU.subtract))
            dve.tensor_copy(toe_hi[:, 0:TOE_FLAT], toe_hi[:, TOE_FLAT:TOE_FLAT + 1].to_broadcast([P, TOE_FLAT]))
            dve.tensor_copy(toe_lo[:, 0:TOE_FLAT], toe_lo[:, TOE_FLAT:TOE_FLAT + 1].to_broadcast([P, TOE_FLAT])).then_inc(s_toe, 1)
            dve.wait_ge(s_toe, 1)
            link(dve.tensor_tensor(flat[:], toe_hi[:, 0:1], toe_lo[:, 0:1], ALU.add))
            dve.tensor_scalar(flat_w[:], cnt_half[:, :, 0:2], flat[:, 0:1], None, ALU.mult)
            link(dve.tensor_scalar(sk_flat[:], sk_half[:, 0:2], flat[:, 0:1], None, ALU.mult))
            dve.wait_ge(s_eg, 3)
            link(dve.tensor_scalar(eg_hi[:], eg[:], ESCALE, None, ALU.mult))
            dve.scalar_tensor_tensor(eg_lo[:], eg[:], ESCALE, eg_hi[:], ALU.mult, ALU.subtract).then_inc(s_egs, 1)
            dve.wait_ge(loads["ids_all"], 16)
            link(dve.tensor_copy(ids_all[:, SEQS * LEN:], ids_all[:, LEN + FIRST:LEN + FIRST + 1]))
            link(dve.memset(ids_all[:, LEN + FIRST:LEN + FIRST + 1], float(SKIP_ID)))
            dve.tensor_scalar(oneh_t[:], ids_all[:], iota_p[:, 0:1], None, ALU.is_equal)
            dve.tensor_scalar(skip_row[:], ids_all[0:1, LEN:], float(SKIP_ID), None, ALU.is_equal).then_inc(s_onet, 1)
            dve.wait_ge(s_qsb, 3)
            for s in range(SEQS):
                dve.tensor_scalar(vh[:, s, :], vp[:, s, :], cnt_half[:, s, 2:3], None, ALU.mult)
            dve.tensor_scalar(vh_skip[:], vp[0:1, 2, :], sk_half[0:1, 2:3], None, ALU.mult)
            dve.tensor_tensor(v_sel[:], ident[0:8, 0:8].unsqueeze(2).to_broadcast([8, 8, D + 1]),
                              bcast(vp[0:8, 2, :], [8, 8, D + 1], 1), ALU.mult).then_inc(s_vh, 1)

            def parts(src, dst, rest):
                link(dve.tensor_copy(dst[:, 0], src))
                link(dve.tensor_tensor(rest[:], src, dst[:, 0], ALU.subtract))
                link(dve.tensor_copy(dst[:, 1], rest[:]))
                link(dve.tensor_tensor(rest[:], rest[:], dst[:, 1], ALU.subtract))
                return dve.tensor_copy(dst[:, 2], rest[:])

            parts(hv[:], hv_part, hv_rest).then_inc(s_hpart, 1)
            dve.wait_ge(loads["ln2"], 48)
            for b in range(2):
                dve.tensor_tensor(h_all[:, b, :], hv[:, 1 - b, :], b2_all[:], ALU.add)
            dve.wait_ge(s_sk, 1)
            link(dve.tensor_copy(sk_a[:], bank[2][:, 8:16]))
            for half in range(2):
                q = slice(NQ * half, NQ * half + NQ)
                ins = dve.scalar_tensor_tensor(sk_p[:, q], bank[2][:, q], sk_flat[:, half:half + 1], sk_a[:, q],
                                               ALU.add, ALU.mult)
            ins.then_inc(s_skp, 1)

            def read_h(t):
                dve.wait_ge(s_u, t + 2)
                b = 2 + NQ * t
                dve.tensor_tensor(h_all[:, b:b + NQ, :], bank[4][:, 0:NQ * D].rearrange("p (b d) -> p b d", d=D),
                                  bcast(b2_all[:, :], [P, NQ, D], 1), ALU.add).then_inc(s_hsb, 1)

            for t in range(4):
                s, half = tile_s(t)
                dve.wait_ge(s_m, t + 1)
                dve.wait_ge(s_asb, t + 1)
                dve.scalar_tensor_tensor(pT[:, t, :], bank[M_BANK[t]][:, :], flat_w[:, s, half:half + 1],
                                         a_sb[:, t % 2, :], ALU.add, ALU.mult).then_inc(s_p, 1)
                if t == 0:
                    dve.wait_ge(s_skT, 1)
                    dve.tensor_copy(sk_pT[:], bank[2][0:8, 0:P]).then_inc(s_skTsb, 1)
                if t >= 1:
                    read_h(t - 1)
            read_h(3)
            dve.wait_ge(loads["w1"], 32)
            dve.wait_ge(loads["gate"], 32)
            dve.wait_ge(loads["gate_b"], 32)
            dve.tensor_scalar(w1_hi[:], w1_sb[:], XSCALE, None, ALU.mult)
            dve.tensor_tensor(gb_sum[:], gb_all[:, 0, :], gb_all[:, 1, :], ALU.add)
            link(dve.tensor_scalar(gate_hi[:], gate_sb[:], XSCALE, None, ALU.mult))
            dve.scalar_tensor_tensor(w1_lo[:].rearrange("p e h -> p (e h)"), w1_sb[:].rearrange("p e h -> p (e h)"), XSCALE,
                                     w1_hi[:].rearrange("p e h -> p (e h)"), ALU.mult, ALU.subtract)
            dve.scalar_tensor_tensor(gate_lo[:], gate_sb[:], XSCALE, gate_hi[:], ALU.mult, ALU.subtract).then_inc(s_w1s, 1)

            def rows(k):
                bs = slice(TRIO * k, TRIO * k + TRIO)
                dve.wait_ge(s_usb, 5)
                link(dve.reciprocal(rden[:], u_all[:, bs, D]))
                for i in range(TRIO):
                    ins = dve.scalar_tensor_tensor(o[:, i, :], u_all[:, TRIO * k + i, 0:D], rden[:, i:i + 1], pb_all[:],
                                                   ALU.mult, ALU.add)
                link(ins)
                row_stats(o, stat, mv, var1, TRIO, 1.0, s_var1)
                dve.wait_ge(s_rs1, k + 1)
                normalise(o, o, mv, rs1, TRIO).then_inc(s_on, 1)
                dve.wait_ge(s_h2, k + 1)
                row_stats(h_all[:, bs, :], stat, mv, var2, TRIO, 1.0 / (XSCALE * XSCALE), s_var2)
                dve.wait_ge(s_rs2, k + 1)
                link(normalise(xn, h_all[:, bs, :], mv, rs2, TRIO))
                if k >= 1:
                    dve.wait_ge(s_xT, k)
                link(dve.tensor_copy(xs[:, :, 0, :], xn[:]))
                dve.tensor_tensor(xs[:, :, 1, :], xn[:], xs[:, :, 0, :], ALU.subtract).then_inc(s_xs, 1)

            def choose(k):
                dve.wait_ge(s_lg, k + 1)
                link(dve.scalar_tensor_tensor(lg[:], bank[4][:, 0:TRIO * EXPERTS].rearrange("p (b e) -> p b e", e=EXPERTS),
                                              1.0 / (XSCALE * XSCALE), bcast(gb_sum[:, :], [P, TRIO, EXPERTS], 1),
                                              ALU.mult, ALU.add))
                for i in range(TRIO):
                    ins = dve.max(top[:, i, :], lg[:, i, :])
                link(ins)
                dve.tensor_tensor(gd[:], top[:, :, 1], top[:, :, 0], ALU.subtract).then_inc(s_gd, 1)
                for i in range(TRIO):
                    ins = dve.max_index(tix[:, i, :], top[:, i, :], lg[:, i, :])
                link(ins)
                dve.tensor_copy(tixf[:], tix[:, :, 0:2])
                dve.wait_ge(s_ge, k + 1)
                link(dve.tensor_scalar(gs[:], ge[:], 1.0, None, ALU.add))
                link(dve.reciprocal(gw[:, 0, :], gs[:]))
                link(dve.tensor_tensor(gw[:, 1, :], gw[:, 0, :], ge[:], ALU.mult))
                for i in range(TRIO):
                    dve.tensor_scalar(c1[:, i, :], iota_row[:, 0:EXPERTS], tixf[:, i, 0:1], gw[:, 0, i:i + 1],
                                      ALU.is_equal, ALU.mult)
                    ins = dve.tensor_scalar(c2[:, i, :], iota_row[:, 0:EXPERTS], tixf[:, i, 1:2], gw[:, 1, i:i + 1],
                                            ALU.is_equal, ALU.mult)
                link(ins)
                dve.tensor_tensor(comb[:], c1[:], c2[:], ALU.add).then_inc(s_comb, 1)

            def combine(k):
                bs = slice(TRIO * k, TRIO * k + TRIO)
                dve.wait_ge(s_cb, k + 1)
                dve.tensor_tensor(res[:], bank[4][:, 0:TRIO * D].rearrange("p (b d) -> p b d", d=D), h_all[:, bs, :],
                                  ALU.add).then_inc(s_res, 1)
                for i in range(TRIO):
                    n = TRIO * k + i
                    dve.wait_ge(s_y, n + 1)
                    dve.tensor_tensor(prod[:, n % 2], bank[5 + i][:, :].rearrange("p (e d) -> p e d", d=D),
                                      comb[:, i, :].unsqueeze(2).to_broadcast([P, EXPERTS, D]), ALU.mult).then_inc(s_prod, 1)
                    dve.wait_ge(s_prod, n + 1)
                    ins = dve.tensor_reduce(acc[:, i, :], prod[:, n % 2].rearrange("p e d -> p d e"), AX.X, ALU.add)
                link(ins)
                dve.tensor_tensor(fin_all[:, bs, :], acc[:], res[:], ALU.add).then_inc(s_fin, 1)

            rows(0)
            for k in range(TRIOS):
                choose(k)
                if k + 1 < TRIOS:
                    rows(k + 1)
                combine(k)
                if k == 0:
                    dve.wait_ge(s_fin, 1)
                    parts(fin_all[:, 0:3, :], fin_part, fin_rest).then_inc(s_fpart, 1)
            dve.wait_ge(s_look, 1)
            dve.tensor_copy(looked[:, 0, :, :], bank[0][:, :].rearrange("p (n d) -> p n d", d=D)).then_inc(s_looked0, 1)

        @block.tensor
        def _(pe_):
            mm = pe_.matmul

            pe_.wait_ge(s_ident, 1)
            pe_.wait_ge(s_ids, 1)
            for s in range(SEQS):
                ins = pe_.transpose(bank[0].bitcast(BF16)[:, ROWS * s:ROWS * s + ROWS], ids_b[:, s, :],
                                    ident_b[0:ROWS, 0:ROWS])
            ins.then_inc(s_idT, 1)
            pe_.wait_ge(s_onej, 1)
            pe_.wait_ge(s_const, 2)
            for s in range(SEQS):
                for c, (a, b) in enumerate(((0, 4), (4, 8), (8, ROWS))):
                    for j in range(a, b):
                        mm(bank[1][:, 3 * s + c:3 * s + c + 1], oneh_j[:, ROWS * s + j, :], ones_h[:, 0:1],
                           start=(j == a), stop=(j == b - 1))
            mm(bank[1][:, 8:8 + ROWS], ones_h[:], skip_j[:], start=True, stop=True).then_inc(s_cnt, 1)
            pe_.wait_ge(s_hl, 1)
            for i in range(3):
                ins = pe_.transpose(bank[2][0:D, P * i:P * i + P], vy[:, i, :], ident[:])
            ins.then_inc(s_hT, 1)
            pe_.wait_ge(s_hTsb, 1)
            pe_.wait_ge(loads["qkv"], 32)
            for i in range(3):
                mm(bank[3 + i][0:D, 0:3 * P], qkv_sb[:, D * i:D * i + D], hvT[:], start=True, stop=True).then_inc(s_qkv, 1)
            pe_.wait_ge(s_qsb, 1)
            pe_.wait_ge(s_ksb, 1)
            pe_.wait_ge(s_absent, 1)
            for i, (a, b, k0) in enumerate(((S0, S1, 0), (S1, SK, P), (SK, GW, P))):
                mm(bank[6][:, a:b], qT[:, P * i:P * i + P], kT[:, k0:k0 + b - a], start=True, stop=False)
                ins = mm(bank[6][:, a:b], ones_b[:], absent_d[:, k0:k0 + b - a], start=False, stop=True)
            ins.then_inc(s_g, 1)
            pe_.wait_ge(s_qsb, 2)
            pe_.wait_ge(loads["proj"], 16)
            for i in range(3):
                ins = mm(bank[2][:, D * i:D * i + D], vT[:, P * i:P * i + P], proj_sb[:], start=True, stop=True)
            ins.then_inc(s_vproj, 1)

            def weights(t):
                s, half = tile_s(t)
                if t == 1:
                    pe_.wait_ge(s_idcol, 1)
                if t == 2:
                    pe_.wait_ge(s_cntread, 1)
                if t == 3:
                    pe_.wait_ge(s_skTsb, 1)
                js = (NQ, 2 * NQ)[half]
                for j in range(js):
                    z = TOE_FLAT + HALF * half - P * j
                    for part, toe in enumerate((toe_hi, toe_lo)):
                        ins = mm(bank[M_BANK[t]][:, :], oneh_j[:, ROWS * s + j, :], toe[:, z:z + HALF],
                                 start=(j == 0 and part == 0), stop=(j == js - 1 and part == 1))
                ins.then_inc(s_m, 1)

            pe_.wait_ge(s_toe, 1)
            weights(0)
            pe_.wait_ge(s_eg, 3)
            for s in range(SEQS):
                pe_.transpose(bank[3][:, P * s:P * s + P], eg[:, P * s:P * s + P], ident[:])
            pe_.transpose(bank[3][0:1, 2 * P:3 * P], eg[:, SK - 1:SK], ident[:]).then_inc(s_egT, 1)
            pe_.wait_ge(loads["eb1"], 16)
            pe_.transpose(bank[4][:, 0:EXPERTS], eb1_sb[:], ident[0:EXPERTS, 0:EXPERTS]).then_inc(s_eb1T, 1)
            weights(1)

            def scores(t):
                s, half = tile_s(t)
                if t >= 2:
                    pe_.wait_ge(s_asb, t - 1)
                q0 = LEN * s + FIRST + HALF * half
                dst = bank[A_BANK[t % 2]][:, :]
                mm(dst, eg_hi[:, P * s:P * s + P], oneh_t[:, q0:q0 + HALF], start=True, stop=False)
                ins = mm(dst, eg_lo[:, P * s:P * s + P], oneh_t[:, q0:q0 + HALF], start=False, stop=(s == 0))
                if s:
                    for part, e in enumerate((eg_hi, eg_lo)):
                        ins = mm(dst, e[0:1, SK:SK + P], skip_row[:, q0 - LEN:q0 - LEN + HALF], start=False, stop=part == 1)
                ins.then_inc(s_a, 1)

            pe_.wait_ge(s_egs, 1)
            pe_.wait_ge(s_onet, 1)
            scores(0)
            scores(1)
            pe_.wait_ge(s_qsb, 3)
            for i in range(2 * NQ):
                js = NQ if i < NQ else 2 * NQ
                for j in range(js):
                    z = TOE_FLAT + P * (i - j)
                    for part, toe in enumerate((toe_hi, toe_lo)):
                        mm(bank[2][:, i:i + 1], toe[:, z:z + P], skip_j[:, j:j + 1],
                           start=(j == 0 and part == 0), stop=(j == js - 1 and part == 1))
            for i in range(2 * NQ):
                q0 = FIRST + P * i
                for part, e in enumerate((eg_hi, eg_lo)):
                    mm(bank[2][:, 8 + i:9 + i], oneh_t[:, LEN + q0:LEN + q0 + P], e[:, SK - 1:SK],
                       start=part == 0, stop=False)
                for part, e in enumerate((eg_hi, eg_lo)):
                    ins = mm(bank[2][:, 8 + i:9 + i], skip_row[:, q0:q0 + P], e[0:1, GW - 1:GW],
                             start=False, stop=part == 1)
            ins.then_inc(s_sk, 1)
            pe_.wait_ge(s_egTsb, 1)
            pe_.wait_ge(s_vh, 1)
            mm(bank[3][:, 0:D + 1], egT[:, 1, :], vh[:, 1, :], start=True, stop=False)
            mm(bank[3][:, 0:D + 1], egT[0:1, 2, :], vh_skip[:], start=False, stop=True)
            mm(bank[3][:, D + 1:2 * (D + 1)], egT[:, 0, :], vh[:, 0, :], start=True, stop=True).then_inc(s_u, 1)
            pe_.wait_ge(s_skp, 1)
            pe_.transpose(bank[2][0:8, 0:P], sk_p[:], ident[:]).then_inc(s_skT, 1)
            weights(2)
            pe_.wait_ge(s_eb1, 1)
            pe_.wait_ge(s_hpart, 1)

            def results(t):
                s, half = tile_s(t)
                pe_.wait_ge(s_p, t + 1)
                pe_.wait_ge(s_usb, t + 1)
                if t >= 1:
                    pe_.wait_ge(s_hsb, t)
                for i in range(NQ):
                    q0 = FIRST + P * (NQ * half + i)
                    u = bank[3][:, (D + 1) * i:(D + 1) * (i + 1)]
                    mm(u, pT[:, t, P * i:P * i + P], vp[:, s, :], start=True, stop=(s == 0))
                    if s:
                        mm(u, sk_pT[:], v_sel[:, NQ * half + i, :], start=False, stop=True)
                    h = bank[4][:, D * i:D * i + D]
                    for part in range(3):
                        ins = mm(h, oneh_t[:, LEN * s + q0:LEN * s + q0 + P], hv_part[:, part, s, :],
                                 start=part == 0, stop=(s == 0 and part == 2))
                    if s:
                        for part in range(3):
                            ins = mm(h, skip_row[:, q0:q0 + P], hv_part[0:1, part, 2, :], start=False, stop=part == 2)
                ins.then_inc(s_u, 1)

            pe_.wait_ge(s_skTsb, 1)
            results(0)
            weights(3)
            scores(2)
            results(1)
            scores(3)
            results(2)
            results(3)
            pe_.wait_ge(s_usb, 5)
            pe_.wait_ge(s_hsb, 4)
            pe_.wait_ge(s_w1s, 1)
            pe_.wait_ge(loads["w2"], 16)
            pe_.wait_ge(loads["eb2"], 16)
            for k in range(TRIOS):
                pe_.wait_ge(s_xs, k + 1)
                if k >= 1:
                    pe_.wait_ge(s_cTsb, k)
                for i in range(TRIO):
                    ins = pe_.transpose(bank[3].bitcast(F16)[:, P * i:P * i + P],
                                        xs[:, i, :, :].rearrange("p a d -> p (a d)"), ident_h[:])
                ins.then_inc(s_xT, 1)
                pe_.wait_ge(s_xTsb, k + 1)
                if k >= 1:
                    pe_.wait_ge(s_res, k)
                for i in range(TRIO):
                    for part, w in enumerate((gate_hi, gate_lo)):
                        ins = mm(bank[4][:, EXPERTS * i:EXPERTS * (i + 1)], xT[:, P * i:P * i + P], w[:],
                                 start=part == 0, stop=part == 1)
                ins.then_inc(s_lg, 1)
                for e in range(EXPERTS):
                    n = EXPERTS * k + e
                    if n >= 3:
                        pe_.wait_ge(s_hid, n - 2)
                    for part, w in enumerate((w1_hi, w1_lo)):
                        ins = mm(bank[n % 3][:, 0:TRIO * P], w[:, e, :], xT[:], start=part == 0, stop=part == 1)
                    ins.then_inc(s_z, 1)
                pe_.wait_ge(s_comb, k + 1)
                for i in range(TRIO):
                    ins = pe_.transpose(bank[3][0:EXPERTS, P * i:P * i + P], comb[:, i, :], ident[:])
                ins.then_inc(s_cT, 1)
                pe_.wait_ge(s_hid, EXPERTS * (k + 1))
                for i in range(TRIO):
                    if k >= 1:
                        pe_.wait_ge(s_prod, TRIO * (k - 1) + i + 1)
                    for e in range(EXPERTS):
                        ins = mm(bank[5 + i][:, D * e:D * e + D], hid[:, e, P * i:P * i + P], w2_sb[:, e, :],
                                 start=True, stop=True)
                    ins.then_inc(s_y, 1)
                    if i == 0:
                        pe_.wait_ge(s_cTsb, k + 1)
                        for b in range(TRIO):
                            ins = mm(bank[4][:, D * b:D * b + D], cT[:, P * b:P * b + P], eb2_sb[:], start=True, stop=True)
                        ins.then_inc(s_cb, 1)
            pe_.wait_ge(s_fpart, 1)
            pe_.wait_ge(s_hid, EXPERTS * TRIOS)

            def look(dst, s, col, n, q):
                for part in range(3):
                    ins = mm(dst, oneh_t[:, col:col + n], fin_part[:, part, 1 - s, :], start=part == 0,
                             stop=(s == 0 and part == 2))
                if s:
                    for part in range(3):
                        ins = mm(dst, skip_row[:, q:q + n], fin_part[0:1, part, 2, :], start=False, stop=part == 2)
                return ins

            for s in range(SEQS):
                for i in range(FIRST // P):
                    ins = look(bank[s][:, D * i:D * i + D], s, LEN * s + P * i, P, P * i)
                ins.then_inc(s_look, 1)
            look(bank[2][0:1, 0:D], 1, SEQS * LEN, 1, LEN).then_inc(s_look, 1)


_INS = ['x', 'L0_tok_token_W', 'L0_tok_pe', 'L0_attn_ln1_g', 'L0_attn_ln1_b', 'L0_attn_qkv_w', 'L0_attn_qkv_b',
        'L0_attn_bias_table', 'L0_attn_scale', 'L0_attn_proj_w', 'L0_attn_proj_b', 'L0_attn_ln2_g', 'L0_attn_ln2_b',
        'L0_ffn_Wg', 'L0_ffn_bg', 'L0_ffn_bias', 'L0_ffn_W1', 'L0_ffn_b1', 'L0_ffn_W2', 'L0_ffn_b2']


def kernel(**inputs):
    import numpy as _np
    import concourse.bacc as _bacc
    from concourse import mybir as _mybir
    from concourse.bass_utils import run_bass_kernel_spmd as _run

    nc = _bacc.Bacc("TRN2", target_bir_lowering=False, num_devices=1)
    arrays, args = {}, []
    for name in _INS:
        a = _np.ascontiguousarray(inputs[name])
        if a.ndim == 0:
            a = a.reshape(1)
        arrays[f"in_{name}_dram"] = a
        args.append(nc.dram_tensor(f"in_{name}_dram", a.shape, _mybir.dt.from_np(a.dtype), kind="ExternalInput").ap())
    args.append(nc.dram_tensor("out_0_dram", (SEQS, LEN, D), F32, kind="ExternalOutput").ap())
    build(nc, *args)
    r = _run(nc, [arrays], core_ids=[0])
    return r.results[0]["out_0_dram"]
```

```python
from contextlib import ExitStack

import concourse.bass as bass
from concourse import mybir

F32 = mybir.dt.float32
F16 = mybir.dt.float16
BF16 = mybir.dt.bfloat16
I32 = mybir.dt.int32
U32 = mybir.dt.uint32
ALU = mybir.AluOpType
ACT = mybir.ActivationFunctionType
AX = mybir.AxisListType

P = 128
VOCAB = 128
D = 64
SEQS, LEN = 2, 2048
ROWS = LEN // P
TABLE = 1023
FIRST = LEN // 2
SEP_ID, PAD_ID = 13, 1
SKIP_ID = 128
EXPERTS, HID = 8, 128
EPS = 1e-5
ABSENT = -1e30
ESCALE = 32768.0
XSCALE = 64.0
HSCALE = 32.0
YSCALE = HSCALE * XSCALE
TOE = 1408
TOE_FLAT = TOE - 1024
NQ = 4
HALF = NQ * P
JBLK = FIRST // P
GROUPS, SIX = 3, 6
BLOCKS = GROUPS * SIX
TRIO = 3
TRIOS = BLOCKS // TRIO
HSLOTS = 4
S0, S1, SK = 0, 128, 257
GW = 386
W1W = EXPERTS * HID + EXPERTS
C_G2, C_B2, C_PB, C_GB, C_SC = 3 * D, 4 * D, 5 * D, 6 * D, 6 * D + 2 * EXPERTS
VECS = C_SC + 1
C_PROJ, C_G1, C_B1 = 3 * D, 4 * D, 4 * D + 1
QW = 4 * D + 2


def build(nc, x, token_w, vecs, qkv, bias_table, w1g, w2b1, b2, out):
    ids_dram = nc.dram_tensor("ids_scratch", (SEQS, LEN), BF16, kind="Internal").ap()

    with ExitStack() as ctx:
        def sb(name, shape, dt=F32):
            return ctx.enter_context(nc.sbuf_tensor(name, shape, dt))

        def sem(name):
            return ctx.enter_context(nc.semaphore(name))

        bank = [ctx.enter_context(nc.psum_tensor(f"bank{i}", [P, 512], F32)) for i in range(8)]

        iota_row = sb("iota_row", [P, P])
        iota_h = sb("iota_h", [P, P], F16)
        iota_p = sb("iota_p", [P, 1])
        ident = sb("ident", [P, P])
        ident_h = sb("ident_h", [P, P], F16)
        ident_b = sb("ident_b", [P, P], BF16)
        ones_h = sb("ones_h", [P, 1], F16)
        ones_b = sb("ones_b", [P, P], BF16)
        neghalf = sb("neghalf", [P, 8])
        ids_i = sb("ids_i", [ROWS, SEQS, P], I32)
        ids_f = sb("ids_f", [ROWS, SEQS, P])
        is_sep = sb("is_sep", [ROWS, P])
        is_pad = sb("is_pad", [ROWS, P])
        ids_b = sb("ids_b", [ROWS, SEQS, P], BF16)
        id_col = sb("id_col", [P, SEQS * ROWS])
        oneh_j = sb("oneh_j", [P, SEQS * JBLK, P], F16)
        skip_j = sb("skip_j", [P, ROWS], F16)
        ids_all = sb("ids_all", [P, SEQS * LEN + 1], BF16)
        oneh_t = sb("oneh_t", [P, SEQS * LEN + 1], F16)
        oneh_junk = sb("oneh_junk", [P, LEN + 1], F16)
        skip_row = sb("skip_row", [1, LEN + 1], F16)
        table_all = sb("table_all", [P, TABLE])
        hankel = sb("hankel", [P, 1024])
        nbmax = sb("nbmax", [P, 1])
        toe_hi = sb("toe_hi", [P, TOE], F16)
        toe_lo = sb("toe_lo", [P, TOE], F16)
        flat = sb("flat", [P, 1])
        w_tok = sb("w_tok", [P, D])
        vec = sb("vec", [P, VECS])
        hv = vec[:, 0:3 * D].rearrange("p (s d) -> p s d", d=D)
        qkv_sb = sb("qkv_sb", [D + 1, QW])
        gb_sum = sb("gb_sum", [P, EXPERTS])
        w1_sb = sb("w1_sb", [P, W1W])
        w1_hi = sb("w1_hi", [P, W1W], F16)
        w1_lo = sb("w1_lo", [P, W1W], F16)
        w2_sb = sb("w2_sb", [P, EXPERTS * D + EXPERTS])
        w2_hi = sb("w2_hi", [P, EXPERTS * D], F16)
        w2_lo = sb("w2_lo", [P, EXPERTS * D], F16)
        b1_col = sb("b1_col", [P, EXPERTS])
        b2_row = sb("b2_row", [1, EXPERTS * D])
        b2_part = sb("b2_part", [1, 3, EXPERTS * D], BF16)
        b2_k = sb("b2_k", [3, EXPERTS * D], BF16)
        pmask = sb("pmask", [P, 1])
        hb = sb("hb", [P, 3, D])
        h_part = sb("h_part", [P, 3, 3, D], BF16)
        vy = sb("vy", [P, 3, D])
        vstat = sb("vstat", [P, 3, 6])
        vmv = sb("vmv", [P, 3, 2])
        vvar = sb("vvar", [P, 3])
        vrs = sb("vrs", [P, 3])
        hvT = sb("hvT", [D + 1, 3 * P])
        qT = sb("qT", [D, 3 * P])
        kT = sb("kT", [D, 3 * P])
        vT = sb("vT", [D, 3 * P])
        vp = sb("vp", [P, 3, D + 1])
        vsum = sb("vsum", [P, 3])
        vmean = sb("vmean", [P, 3])
        vh = sb("vh", [P, SEQS, D + 1])
        vh_skip = sb("vh_skip", [1, D + 1])
        v_sel = sb("v_sel", [8, 8, D + 1])
        cnt_late = sb("cnt_late", [P, SEQS])
        cnt = sb("cnt", [P, SEQS, 2])
        cnt_half = sb("cnt_half", [P, SEQS, 3])
        skc = sb("skc", [P, ROWS])
        sk_half = sb("sk_half", [P, 3])
        flat_w = sb("flat_w", [P, SEQS, 2])
        sk_flat = sb("sk_flat", [P, 2])
        absent = sb("absent", [P, 3])
        absent_d = sb("absent_d", [P, 257], BF16)
        gmax = sb("gmax", [P, 3])
        eg = sb("eg", [P, GW])
        eg_hi = sb("eg_hi", [P, GW], F16)
        eg_lo = sb("eg_lo", [P, GW], F16)
        egT = sb("egT", [P, 3, P])
        a_sb = sb("a_sb", [P, 2, HALF])
        pT = sb("pT", [P, 4, HALF])
        sk_a = sb("sk_a", [P, 8])
        sk_p = sb("sk_p", [P, 8])
        sk_pT = sb("sk_pT", [8, P])
        h_all = sb("h_all", [P, BLOCKS, D])
        fin_all = sb("fin_all", [P, BLOCKS, D])
        usq = sb("usq", [P, SIX, D])
        uss = sb("uss", [P, SIX])
        dens = sb("dens", [P, SIX])
        deps = sb("deps", [P, SIX])
        var1 = sb("var1", [P, SIX])
        rs1 = sb("rs1", [P, SIX])
        on = sb("on", [P, SIX, D])
        og = sb("og", [P, SIX, D])
        stat = sb("stat", [P, SIX, 6])
        mv = sb("mv", [P, SIX, 2])
        var2 = sb("var2", [P, SIX])
        rs2 = sb("rs2", [P, SIX])
        xc = sb("xc", [P, SIX, D])
        xn = sb("xn", [P, SIX, D])
        xs = sb("xs", [P, 2, SIX, 2, D], F16)
        xT = sb("xT", [P, 2, SIX * P], F16)
        lg = sb("lg", [P, SIX, EXPERTS])
        top = sb("top", [P, SIX, 8])
        tix = sb("tix", [P, SIX, 8], U32)
        tixf = sb("tixf", [P, 2, SIX])
        gd = sb("gd", [P, SIX])
        ge = sb("ge", [P, SIX])
        gs = sb("gs", [P, SIX])
        gw = sb("gw", [P, 2, SIX])
        sel = sb("sel", [P, 2, SIX, EXPERTS])
        comb = sb("comb", [P, 2, SIX, EXPERTS])
        hid = sb("hid", [P, HSLOTS, TRIO * P])
        hid_hi = sb("hid_hi", [P, 2, EXPERTS, TRIO * P], F16)
        hid_lo = sb("hid_lo", [P, 2, EXPERTS, TRIO * P], F16)
        prod = sb("prod", [P, 2, EXPERTS, D])
        acc = sb("acc", [P, TRIO, D])
        fin_part = sb("fin_part", [P, 3, 3, D], BF16)
        looked = sb("looked", [P, SEQS, 8, D])
        looked1 = sb("looked1", [1, D])
        rest = sb("rest", [P, 8 * D])

        loads = {n: sem("ld_" + n) for n in (
            "ids", "table", "hankel", "scratch", "ids_all", "w_tok", "vecs", "qkv", "w1", "w2", "b2", "b2_k")}
        s_const = sem("s_const")
        s_dve = sem("s_dve")
        s_pool = sem("s_pool")
        s_act = sem("s_act")
        s_ident = sem("s_ident")
        s_ids = sem("s_ids")
        s_idT = sem("s_idT")
        s_idcol = sem("s_idcol")
        s_onej = sem("s_onej")
        s_cnt = sem("s_cnt")
        s_cntread = sem("s_cntread")
        s_cntlate = sem("s_cntlate")
        s_absent = sem("s_absent")
        s_onet = sem("s_onet")
        s_skrow = sem("s_skrow")
        s_nbmax = sem("s_nbmax")
        s_expb = sem("s_expb")
        s_toe = sem("s_toe")
        s_hv = sem("s_hv")
        s_vvar = sem("s_vvar")
        s_vrs = sem("s_vrs")
        s_hl = sem("s_hl")
        s_hT = sem("s_hT")
        s_hTsb = sem("s_hTsb")
        s_qkv = sem("s_qkv")
        s_qsb = sem("s_qsb")
        s_ksb = sem("s_ksb")
        s_vproj = sem("s_vproj")
        s_vp = sem("s_vp")
        s_g = sem("s_g")
        s_gmax = sem("s_gmax")
        s_eg = sem("s_eg")
        s_egs = sem("s_egs")
        s_egT = sem("s_egT")
        s_egTsb = sem("s_egTsb")
        s_vh = sem("s_vh")
        s_hb = sem("s_hb")
        s_w1s = sem("s_w1s")
        s_b2p = sem("s_b2p")
        s_m = sem("s_m")
        s_a = sem("s_a")
        s_asb = sem("s_asb")
        s_p = sem("s_p")
        s_sk = sem("s_sk")
        s_skp = sem("s_skp")
        s_skT = sem("s_skT")
        s_skTsb = sem("s_skTsb")
        s_u = sem("s_u")
        s_usq = sem("s_usq")
        s_var1 = sem("s_var1")
        s_rs1 = sem("s_rs1")
        s_h2 = sem("s_h2")
        s_var2 = sem("s_var2")
        s_rs2 = sem("s_rs2")
        s_xs = sem("s_xs")
        s_xT = sem("s_xT")
        s_xTsb = sem("s_xTsb")
        s_lg = sem("s_lg")
        s_lgread = sem("s_lgread")
        s_gd = sem("s_gd")
        s_ge = sem("s_ge")
        s_z = sem("s_z")
        s_hid = sem("s_hid")
        s_lo_d = sem("s_lo_d")
        s_lo_p = sem("s_lo_p")
        s_w2s = sem("s_w2s")
        s_y = sem("s_y")
        s_prod = sem("s_prod")
        s_fin = sem("s_fin")
        s_fpart = sem("s_fpart")
        s_look = sem("s_look")
        s_looked = sem("s_looked")
        s_out = sem("s_out")

        def bcast(ap, shape, axis):
            return ap.unsqueeze(axis).to_broadcast(shape)

        def tile_s(t):
            return 1 - t // 2, t % 2

        LO_DVE = (3, 5)
        LO_POOL = tuple(e for e in range(EXPERTS) if e not in LO_DVE)

        def wait_lo(eng, n):
            k, e = n // EXPERTS, n % EXPERTS
            if e in LO_DVE:
                eng.wait_ge(s_lo_d, len(LO_DVE) * k + LO_DVE.index(e) + 1)
            else:
                eng.wait_ge(s_lo_p, len(LO_POOL) * k + LO_POOL.index(e) + 1)

        def low_part(eng, k, e):
            n = EXPERTS * k + e
            eng.wait_ge(s_hid, n + 1)
            if k >= 2:
                eng.wait_ge(s_y, TRIO * (k - 1))
            return eng.tensor_tensor(hid_lo[:, k % 2, e, :], hid[:, n % HSLOTS, :], hid_hi[:, k % 2, e, :], ALU.subtract)

        M_BANK = [7, 0, 1, 2]
        A_BANK = [5, 6]
        Y_BANK = [6, 7]
        bank5h = bank[5].bitcast(F16)
        LOGITS = bank[5][:, 448:448 + SIX * EXPERTS]

        class Chain:

            def __init__(self, eng, s):
                self.eng, self.s, self.n = eng, s, 0

            def link(self, ins):
                self.n += 1
                ins.then_inc(self.s, 1)
                self.eng.wait_ge(self.s, self.n)

        block = ctx.enter_context(nc.Block())

        @block.sync
        def _(sp):
            sp.dma_start(ids_i[:], x.rearrange("s (r p) -> r s p", p=P)).then_inc(loads["ids"], 16)
            sp.dma_start(vec[:], vecs.partition_broadcast(P)).then_inc(loads["vecs"], 16)
            sp.dma_start(table_all[:], bias_table[0:TABLE].partition_broadcast(P)).then_inc(loads["table"], 16)
            sp.dma_start(hankel[:], bass.AP(bias_table.tensor, 0, [[1, P], [1, 1024]])).then_inc(loads["hankel"], 16)
            sp.wait_ge(s_ids, 1)
            sp.dma_start(ids_dram.rearrange("s (r p) -> r s p", p=P), ids_b[:]).then_inc(loads["scratch"], 16)
            sp.wait_ge(loads["scratch"], 16)
            sp.dma_start(ids_all[:, 0:SEQS * LEN],
                         ids_dram.rearrange("s n -> (s n)").partition_broadcast(P)).then_inc(loads["ids_all"], 16)
            sp.dma_start(w1_sb[:], w1g).then_inc(loads["w1"], 16)
            sp.dma_start(b2_row[:], b2).then_inc(loads["b2"], 16)
            sp.dma_start(w2_sb[:], w2b1).then_inc(loads["w2"], 16)
            sp.wait_ge(s_b2p, 1)
            sp.dma_start(b2_k[:], b2_part[:]).then_inc(loads["b2_k"], 16)
            stores = 0

            def store(dst, src):
                sp.dma_start(dst, src).then_inc(s_out, 16)

            def rows_of(s, b, n):
                r0 = FIRST + P * (b - (2 if s else 10))
                return out[s, r0:r0 + P * n, :].rearrange("(b p) d -> p b d", p=P)

            for k in range(TRIOS):
                sp.wait_ge(s_fin, k + 1)
                b = TRIO * k
                if k == 0:
                    store(out[1, FIRST + 1:FIRST + P, :], fin_all[1:P, 2, :])
                elif b < 10 < b + TRIO:
                    store(rows_of(1, b, 10 - b), fin_all[:, b:10, :])
                    store(rows_of(0, 10, b + TRIO - 10), fin_all[:, 10:b + TRIO, :])
                    stores += 1
                else:
                    store(rows_of(int(b < 10), b, TRIO), fin_all[:, b:b + TRIO, :])
                stores += 1
                if k == 4:
                    for s in range(SEQS):
                        sp.wait_ge(s_looked, s + 1)
                        store(out[s, 0:FIRST, :].rearrange("(n p) d -> p n d", p=P), looked[:, s, :, :])
                    sp.wait_ge(s_looked, 3)
                    store(out[1, FIRST:FIRST + 1, :], looked1[:])
                    stores += 3
            sp.wait_ge(s_out, 16 * stores)

        @block.gpsimd
        def _(pool):
            ch = Chain(pool, s_pool)
            link = ch.link
            pool.iota(iota_row[:], [[1, P]], base=0, channel_multiplier=0,
                      allow_small_or_imprecise_dtypes=True)
            pool.iota(iota_p[:], [[0, 1]], base=0, channel_multiplier=1,
                      allow_small_or_imprecise_dtypes=True).then_inc(s_const, 1)
            pool.memset(neghalf[:], -0.5)
            pool.memset(vp[:], 1.0)
            pool.memset(ones_h[:], 1.0)
            pool.memset(ones_b[:], 1.0).then_inc(s_const, 1)
            pool.wait_ge(s_const, 2)
            for n in range(2):
                pool.wait_ge(s_vvar, n + 1)
                pool.tensor_tensor(vrs[:], vvar[:], neghalf[:, 0:3], ALU.pow).then_inc(s_vrs, 1)

            def parts(src, dst, left):
                link(pool.tensor_copy(dst(0), src))
                link(pool.tensor_tensor(left, src, dst(0), ALU.subtract))
                link(pool.tensor_copy(dst(1), left))
                link(pool.tensor_tensor(left, left, dst(1), ALU.subtract))
                return pool.tensor_copy(dst(2), left)

            rest3 = rest[:, 0:3 * D].rearrange("p (s d) -> p s d", d=D)
            pool.wait_ge(s_hv, 1)
            link(pool.tensor_tensor(hb[:], hv, bcast(vec[:, C_B2:C_B2 + D], [P, 3, D], 1), ALU.add))
            parts(hb[:], lambda i: h_part[:, i], rest3).then_inc(s_hb, 1)
            pool.wait_ge(loads["w1"], 16)
            link(pool.tensor_scalar(w1_sb[:], w1_sb[:], XSCALE, 0.0, ALU.mult, ALU.add))
            link(pool.tensor_copy(w1_hi[:], w1_sb[:]))
            pool.tensor_tensor(w1_lo[:], w1_sb[:], w1_hi[:], ALU.subtract).then_inc(s_w1s, 1)
            pool.wait_ge(loads["b2"], 16)
            pool.wait_ge(s_hb, 1)
            link(pool.tensor_scalar(b2_row[:], b2_row[:], YSCALE, 0.0, ALU.mult, ALU.add))
            parts(b2_row[:], lambda i: b2_part[:, i], rest[0:1, :]).then_inc(s_b2p, 1)
            pool.wait_ge(loads["w2"], 16)
            pool.tensor_scalar(b1_col[:], w2_sb[:, EXPERTS * D:], HSCALE, 0.0, ALU.mult, ALU.add)
            w2 = w2_sb[:, 0:EXPERTS * D]
            link(pool.tensor_scalar(w2, w2, XSCALE, 0.0, ALU.mult, ALU.add))
            link(pool.tensor_copy(w2_hi[:], w2))
            pool.tensor_tensor(w2_lo[:], w2, w2_hi[:], ALU.subtract).then_inc(s_w2s, 1)

            def rsqrt1(g):
                pool.wait_ge(s_var1, g + 1)
                pool.tensor_tensor(rs1[:], var1[:], neghalf[:, 0:SIX], ALU.pow).then_inc(s_rs1, 1)

            def rsqrt2(g):
                pool.wait_ge(s_var2, g + 1)
                pool.tensor_tensor(rs2[:], var2[:], neghalf[:, 0:SIX], ALU.pow).then_inc(s_rs2, 1)

            rsqrt1(0)
            rsqrt2(0)
            for k in range(TRIOS):
                for e in LO_POOL:
                    low_part(pool, k, e).then_inc(s_lo_p, 1)
                    if (k, e) in ((0, 4), (2, 4)):
                        rsqrt1(k // 2 + 1)
                    if (k, e) in ((1, 0), (3, 0)):
                        rsqrt2(k // 2 + 1)
                if k == 2:
                    pool.wait_ge(s_fin, 1)
                    pool.wait_ge(s_b2p, 1)
                    parts(fin_all[:, 0:3, :], lambda i: fin_part[:, i], rest3).then_inc(s_fpart, 1)

        @block.scalar
        def _(act):
            act.dma_start(w_tok[:], token_w).then_inc(loads["w_tok"], 16)
            act.dma_start(qkv_sb[:], qkv).then_inc(loads["qkv"], 16)
            act.preload_act_table(ACT.Exp)
            act.wait_ge(loads["hankel"], 16)
            act.wait_ge(s_nbmax, 1)
            act.activation(hankel[:], hankel[:], ACT.Exp, bias=nbmax[:, 0:1]).then_inc(s_expb, 1)
            act.wait_ge(s_hT, 1)
            act.wait_ge(loads["qkv"], 16)
            act.activation(hvT[0:D, :], bank[2][0:D, 0:3 * P], ACT.Identity, bias=qkv_sb[0:D, C_B1:C_B1 + 1],
                           scale=qkv_sb[0:D, C_G1:C_G1 + 1]).then_inc(s_hTsb, 1)
            act.wait_ge(s_onet, 1)
            for s in range(SEQS):
                act.activation(oneh_junk[:, FIRST * s:FIRST * (s + 1) + s], oneh_t[:, LEN * s + FIRST:LEN * (s + 1) + s], ACT.Copy,
                               accum_out=cnt_late[:, s:s + 1]).then_inc(s_cntlate, 1)
            act.wait_ge(s_qkv, 1)
            act.copy(qT[:], bank[3][0:D, 0:3 * P]).then_inc(s_qsb, 1)
            act.wait_ge(s_qkv, 3)
            act.copy(vT[:], bank[5][0:D, 0:3 * P]).then_inc(s_qsb, 1)
            act.wait_ge(s_gmax, 1)
            for n, (a, b) in enumerate(((S0, S1), (S1, SK), (SK, GW))):
                act.activation(eg[:, a:b], bank[6][:, a:b], ACT.Exp, bias=gmax[:, n:n + 1]).then_inc(s_eg, 1)
            act.wait_ge(s_egT, 1)
            act.copy(egT[:, 0:2, :], bank[3][:, 0:2 * P].rearrange("p (s d) -> p s d", d=P))
            act.copy(egT[0:1, 2, :], bank[3][0:1, 2 * P:3 * P]).then_inc(s_egTsb, 1)

            def squares(g):
                act.wait_ge(s_u, g + 1)
                if g >= 1:
                    act.wait_ge(s_var1, g)
                act.activation(usq[:], bank[3][:, 0:SIX * (D + 1)].rearrange("p (b d) -> p b d", d=D + 1)[:, :, 0:D],
                               ACT.Square).then_inc(s_usq, 1)

            for t in range(4):
                act.wait_ge(s_a, t + 1)
                if t >= 2:
                    act.wait_ge(s_p, t - 1)
                act.copy(a_sb[:, t % 2, :], bank[A_BANK[t % 2]][:, :]).then_inc(s_asb, 1)
                if t == 1:
                    squares(0)
            act.wait_ge(s_w2s, 1)
            for k in range(TRIOS):
                g = k // 2
                if k % 2 == 0:
                    act.wait_ge(s_xT, g + 1)
                    act.copy(xT[:, g % 2, :], bank5h[:, 0:SIX * P]).then_inc(s_xTsb, 1)
                for e in range(EXPERTS):
                    n = EXPERTS * k + e
                    act.wait_ge(s_z, n + 1)
                    if n >= HSLOTS:
                        wait_lo(act, n - HSLOTS)
                    if k >= 2:
                        act.wait_ge(s_y, TRIO * (k - 1))
                    for dst in (hid[:, n % HSLOTS, :], hid_hi[:, k % 2, e, :]):
                        ins = act.activation(dst, bank[n % 3][:, 0:TRIO * P], ACT.Relu, bias=b1_col[:, e:e + 1],
                                             scale=HSCALE / (XSCALE * XSCALE))
                    ins.then_inc(s_hid, 1)
                    if k % 2 == 0 and e == 0:
                        act.wait_ge(s_gd, g + 1)
                        act.activation(ge[:], gd[:], ACT.Exp).then_inc(s_ge, 1)
                    if k in (0, 2) and e == 3:
                        squares(g + 1)
                    if k == 5 and e in (0, 3, 6):
                        n = (0, 3, 6).index(e)
                        act.wait_ge(s_look, n + 1)
                        if n < 2:
                            act.copy(looked[:, n, :, :], bank[5][:, :].rearrange("p (n d) -> p n d", d=D)).then_inc(s_looked, 1)
                        else:
                            act.copy(looked1[:], bank[5][0:1, 0:D]).then_inc(s_looked, 1)

        @block.vector
        def _(dve):
            ch = Chain(dve, s_dve)
            link = ch.link

            dve.memset(hvT[D:D + 1, :], 1.0)
            dve.wait_ge(s_const, 1)
            dve.tensor_scalar(ident_b[:], iota_row[:], iota_p[:, 0:1], None, ALU.is_equal)
            dve.tensor_copy(iota_h[:], iota_row[:])
            dve.tensor_scalar(pmask[:], iota_p[:], 1.0, None, ALU.min).then_inc(s_ident, 1)
            dve.tensor_scalar(ident[:], iota_row[:], iota_p[:, 0:1], None, ALU.is_equal)
            dve.tensor_scalar(ident_h[:], iota_row[:], iota_p[:, 0:1], None, ALU.is_equal).then_inc(s_ident, 1)
            dve.wait_ge(loads["ids"], 16)
            link(dve.tensor_copy(ids_f[:], ids_i[:]))
            dve.tensor_scalar(is_sep[:], ids_f[:, 0, :], float(SEP_ID), float(SKIP_ID - PAD_ID), ALU.is_equal, ALU.mult)
            link(dve.tensor_scalar(is_pad[:], ids_f[:, 1, :], float(PAD_ID), None, ALU.is_equal))
            link(dve.tensor_tensor(is_pad[:], is_pad[:], is_sep[:], ALU.mult))
            dve.tensor_copy(ids_b[:, 0, :], ids_f[:, 0, :])
            dve.tensor_tensor(ids_b[:, 1, :], ids_f[:, 1, :], is_pad[:], ALU.add).then_inc(s_ids, 1)
            dve.wait_ge(s_ident, 1)
            dve.wait_ge(loads["w_tok"], 16)
            dve.wait_ge(loads["vecs"], 16)
            dve.scalar_tensor_tensor(hv[:, 0, :], w_tok[:], pmask[:, 0:1], hv[:, 0, :], ALU.mult, ALU.add)
            dve.scalar_tensor_tensor(hv[:, 1, :], w_tok[:], pmask[:, 0:1], hv[:, 1, :], ALU.mult, ALU.add).then_inc(s_hv, 1)
            dve.wait_ge(s_hv, 1)

            def row_stats(src, stats, means, var, n, mul, add, signal):
                for i in range(n):
                    ins = dve.bn_stats(stats[:, i, :], src[:, i, :])
                link(ins)
                for i in range(n):
                    ins = dve.bn_aggr(means[:, i, :], stats[:, i, :])
                link(ins)
                dve.tensor_scalar(var[:], means[:, :, 1], mul, add, ALU.mult, ALU.add).then_inc(signal, 1)

            def centre(dst, src, means, n):
                return dve.tensor_tensor(dst, src, means[:, :, 0].unsqueeze(2).to_broadcast([P, n, D]), ALU.subtract)

            def rescale(dst, src, rs, n):
                return dve.tensor_tensor(dst, src, rs[:].unsqueeze(2).to_broadcast([P, n, D]), ALU.mult)

            row_stats(hv, vstat, vmv, vvar, 3, 1.0, EPS, s_vvar)
            link(centre(vy[:], hv, vmv, 3))
            dve.wait_ge(s_idT, 1)
            dve.tensor_copy(id_col[:], bank[0].bitcast(BF16)[:, 0:2 * ROWS]).then_inc(s_idcol, 1)
            dve.wait_ge(s_idcol, 1)

            def one_hots(s, a, b):
                for c in range(a, b):
                    ins = dve.tensor_scalar(oneh_j[:, JBLK * s + c, :], iota_h[:], id_col[:, ROWS * s + c:ROWS * s + c + 1],
                                            None, ALU.is_equal)
                return ins

            one_hots(1, 0, 3)
            dve.wait_ge(s_vrs, 1)
            link(rescale(vy[:], vy[:], vrs, 3))
            row_stats(vy, vstat, vmv, vvar, 3, 1.0, EPS, s_vvar)
            link(centre(vy[:], vy[:], vmv, 3))
            one_hots(1, 3, 6)
            dve.wait_ge(s_vrs, 2)
            rescale(vy[:], vy[:], vrs, 3).then_inc(s_hl, 1)
            dve.wait_ge(loads["table"], 16)
            link(dve.tensor_reduce(nbmax[:], table_all[:], AX.X, ALU.max))
            dve.tensor_scalar(nbmax[:], nbmax[:], -1.0, None, ALU.mult).then_inc(s_nbmax, 1)
            dve.tensor_scalar(skip_j[:], id_col[:, ROWS:2 * ROWS], float(SKIP_ID), None, ALU.is_equal)
            one_hots(1, 6, JBLK).then_inc(s_onej, 1)
            one_hots(0, 0, JBLK).then_inc(s_onej, 1)
            dve.wait_ge(loads["ids_all"], 16)
            link(dve.tensor_copy(ids_all[:, SEQS * LEN:], ids_all[:, LEN + FIRST:LEN + FIRST + 1]))
            link(dve.memset(ids_all[:, LEN + FIRST:LEN + FIRST + 1], float(SKIP_ID)))
            dve.tensor_scalar(oneh_t[:], ids_all[:], iota_p[:, 0:1], None, ALU.is_equal).then_inc(s_onet, 1)
            dve.wait_ge(s_qkv, 2)
            dve.tensor_copy(kT[:], bank[4][0:D, 0:3 * P]).then_inc(s_ksb, 1)
            dve.wait_ge(s_cnt, 1)
            dve.tensor_copy(cnt[:].rearrange("p s c -> p (s c)"), bank[1][:, 0:4])
            dve.tensor_copy(skc[:], bank[1][:, 8:8 + ROWS]).then_inc(s_cntread, 1)
            dve.wait_ge(s_cntread, 1)
            dve.tensor_reduce(sk_half[:, 0:1], skc[:, NQ:ROWS], AX.X, ALU.add)
            dve.tensor_reduce(sk_half[:, 1:2], skc[:, 2 * NQ:ROWS], AX.X, ALU.add)
            dve.tensor_reduce(sk_half[:, 2:3], skc[:], AX.X, ALU.add)
            dve.wait_ge(s_cntlate, SEQS)
            dve.tensor_copy(cnt_half[:, :, 1], cnt_late[:])
            link(dve.tensor_tensor(cnt_half[:, :, 0], cnt[:, :, 1], cnt_late[:], ALU.add))
            link(dve.tensor_tensor(cnt_half[:, :, 2], cnt[:, :, 0], cnt_half[:, :, 0], ALU.add))
            dve.tensor_scalar(absent[:, 0:2], cnt_half[:, :, 2], 0.0, ABSENT, ALU.is_equal, ALU.mult)
            link(dve.tensor_scalar(absent[:, 2:3], sk_half[:, 2:3], 0.0, ABSENT, ALU.is_equal, ALU.mult))
            dve.tensor_scalar(absent_d[:, 0:P], ident[:], absent[:, 0:1], None, ALU.mult)
            dve.tensor_scalar(absent_d[:, P:2 * P], ident[:], absent[:, 1:2], None, ALU.mult)
            dve.tensor_scalar(absent_d[:, 2 * P:2 * P + 1], ident[:, 0:1], absent[:, 2:3], None, ALU.mult).then_inc(s_absent, 1)
            dve.wait_ge(s_expb, 1)
            link(dve.tensor_scalar(toe_hi[:, TOE_FLAT:TOE], hankel[:, ::-1], ESCALE, None, ALU.mult))
            link(dve.scalar_tensor_tensor(toe_lo[:, TOE_FLAT:TOE], hankel[:, ::-1], ESCALE, toe_hi[:, TOE_FLAT:TOE],
                                          ALU.mult, ALU.subtract))
            dve.tensor_copy(toe_hi[:, 0:TOE_FLAT], toe_hi[:, TOE_FLAT:TOE_FLAT + 1].to_broadcast([P, TOE_FLAT]))
            dve.tensor_copy(toe_lo[:, 0:TOE_FLAT], toe_lo[:, TOE_FLAT:TOE_FLAT + 1].to_broadcast([P, TOE_FLAT])).then_inc(s_toe, 1)
            dve.wait_ge(s_g, 1)
            for n, (a, b) in enumerate(((S0, S1), (S1, SK), (SK, GW))):
                ins = dve.tensor_reduce(gmax[:, n:n + 1], bank[6][:, a:b], AX.X, ALU.max)
            link(ins)
            dve.tensor_scalar(gmax[:], gmax[:], -1.0, None, ALU.mult).then_inc(s_gmax, 1)
            dve.tensor_scalar(skip_row[:], ids_all[0:1, LEN:], float(SKIP_ID), None, ALU.is_equal).then_inc(s_skrow, 1)
            dve.wait_ge(s_toe, 1)
            link(dve.tensor_tensor(flat[:], toe_hi[:, 0:1], toe_lo[:, 0:1], ALU.add))
            dve.wait_ge(s_eg, 3)
            link(dve.tensor_scalar(eg_hi[:], eg[:], ESCALE, None, ALU.mult))
            dve.scalar_tensor_tensor(eg_lo[:], eg[:], ESCALE, eg_hi[:], ALU.mult, ALU.subtract).then_inc(s_egs, 1)
            dve.tensor_scalar(flat_w[:], cnt_half[:, :, 0:2], flat[:, 0:1], None, ALU.mult)
            dve.tensor_scalar(sk_flat[:], sk_half[:, 0:2], flat[:, 0:1], None, ALU.mult)
            dve.wait_ge(s_vproj, 1)
            dve.scalar_tensor_tensor(vp[:, :, 0:D], bank[2][:, 0:3 * D].rearrange("p (s d) -> p s d", d=D),
                                     vec[:, C_SC:C_SC + 1], bcast(vec[:, C_PB:C_PB + D], [P, 3, D], 1),
                                     ALU.mult, ALU.add).then_inc(s_vp, 1)
            dve.wait_ge(s_vp, 1)
            link(dve.tensor_reduce(vsum[:], vp[:, :, 0:D], AX.X, ALU.add))
            link(dve.tensor_scalar(vmean[:], vsum[:], 1.0 / D, None, ALU.mult))
            dve.tensor_tensor(vp[:, :, 0:D], vp[:, :, 0:D], vmean[:].unsqueeze(2).to_broadcast([P, 3, D]),
                              ALU.subtract).then_inc(s_vp, 1)
            dve.wait_ge(s_vp, 2)
            for s in range(SEQS):
                dve.tensor_scalar(vh[:, s, :], vp[:, s, :], cnt_half[:, s, 2:3], None, ALU.mult)
            dve.tensor_scalar(vh_skip[:], vp[0:1, 2, :], sk_half[0:1, 2:3], None, ALU.mult)
            dve.tensor_tensor(v_sel[:], ident[0:8, 0:8].unsqueeze(2).to_broadcast([8, 8, D + 1]),
                              bcast(vp[0:8, 2, :], [8, 8, D + 1], 1), ALU.mult).then_inc(s_vh, 1)

            def key_part(t):
                s, half = tile_s(t)
                dve.wait_ge(s_m, t + 1)
                dve.wait_ge(s_asb, t + 1)
                dve.scalar_tensor_tensor(pT[:, t, :], bank[M_BANK[t]][:, :], flat_w[:, s, half:half + 1],
                                         a_sb[:, t % 2, :], ALU.add, ALU.mult).then_inc(s_p, 1)

            U = bank[3][:, 0:SIX * (D + 1)].rearrange("p (b d) -> p b d", d=D + 1)
            H = bank[4][:, 0:SIX * D].rearrange("p (b d) -> p b d", d=D)

            def rows_a(g):
                dve.wait_ge(s_usq, g + 1)
                link(dve.tensor_copy(dens[:], U[:, :, D]))
                dve.scalar_tensor_tensor(deps[:], dens[:], EPS, dens[:], ALU.mult, ALU.mult)
                link(dve.tensor_reduce(uss[:], usq[:], AX.X, ALU.add))
                dve.scalar_tensor_tensor(var1[:], uss[:], 1.0 / D, deps[:], ALU.mult, ALU.add).then_inc(s_var1, 1)

            def rows_b(g):
                hg = h_all[:, SIX * g:SIX * (g + 1), :]
                dve.wait_ge(s_rs1, g + 1)
                link(rescale(on[:], U[:, :, 0:D], rs1, SIX))
                link(dve.tensor_tensor(og[:], on[:], bcast(vec[:, C_G2:C_G2 + D], [P, SIX, D], 1), ALU.mult))
                dve.tensor_tensor(hg, og[:], H, ALU.add).then_inc(s_h2, 1)
                dve.wait_ge(s_h2, g + 1)
                row_stats(hg, stat, mv, var2, SIX, 1.0 / (XSCALE * XSCALE), EPS / (XSCALE * XSCALE), s_var2)
                link(centre(xc[:], hg, mv, SIX))

            def rows_c(g):
                dve.wait_ge(s_rs2, g + 1)
                link(rescale(xn[:], xc[:], rs2, SIX))
                if g >= 2:
                    dve.wait_ge(s_xT, g - 1)
                link(dve.tensor_copy(xs[:, g % 2, :, 0, :], xn[:]))
                dve.tensor_tensor(xs[:, g % 2, :, 1, :], xn[:], xs[:, g % 2, :, 0, :], ALU.subtract).then_inc(s_xs, 1)

            def choose_a(g):
                dve.wait_ge(s_lg, g + 1)
                dve.scalar_tensor_tensor(lg[:], LOGITS.rearrange("p (b e) -> p b e", e=EXPERTS),
                                         1.0 / (XSCALE * XSCALE), bcast(gb_sum[:, :], [P, SIX, EXPERTS], 1),
                                         ALU.mult, ALU.add).then_inc(s_lgread, 1)
                dve.wait_ge(s_lgread, g + 1)
                for i in range(SIX):
                    ins = dve.max(top[:, i, :], lg[:, i, :])
                link(ins)
                dve.tensor_tensor(gd[:], top[:, :, 1], top[:, :, 0], ALU.subtract).then_inc(s_gd, 1)
                for i in range(SIX):
                    ins = dve.max_index(tix[:, i, :], top[:, i, :], lg[:, i, :])
                link(ins)
                dve.tensor_copy(tixf[:], tix[:, :, 0:2].rearrange("p b j -> p j b"))

            def choose_b(g):
                dve.wait_ge(s_ge, g + 1)
                link(dve.tensor_scalar(gs[:], ge[:], 1.0, YSCALE, ALU.add, ALU.mult))
                link(dve.reciprocal(gw[:, 0, :], gs[:]))
                dve.tensor_tensor(gw[:, 1, :], gw[:, 0, :], ge[:], ALU.mult)
                four = [P, 2, SIX, EXPERTS]
                link(dve.tensor_tensor(sel[:], iota_row[:, 0:EXPERTS].unsqueeze(1).unsqueeze(1).to_broadcast(four),
                                       tixf[:].unsqueeze(3).to_broadcast(four), ALU.is_equal))
                link(dve.tensor_tensor(sel[:], sel[:], gw[:].unsqueeze(3).to_broadcast(four), ALU.mult))
                link(dve.tensor_tensor(comb[:, g % 2], sel[:, 0], sel[:, 1], ALU.add))

            def combine(n):
                i, b = n % TRIO, n % SIX
                dve.wait_ge(s_y, n + 1)
                dve.tensor_tensor(prod[:, n % 2], bank[Y_BANK[n % 2]][:, :].rearrange("p (e d) -> p e d", d=D),
                                  comb[:, n // SIX % 2, b, :].unsqueeze(2).to_broadcast([P, EXPERTS, D]), ALU.mult).then_inc(s_prod, 1)
                dve.wait_ge(s_prod, n + 1)
                link(dve.tensor_reduce(acc[:, i, :], prod[:, n % 2].rearrange("p e d -> p d e"), AX.X, ALU.add))
                if i == TRIO - 1:
                    bs = slice(n - TRIO + 1, n + 1)
                    dve.tensor_tensor(fin_all[:, bs, :], acc[:], h_all[:, bs, :], ALU.add).then_inc(s_fin, 1)

            key_part(0)
            dve.wait_ge(s_sk, 1)
            link(dve.tensor_copy(sk_a[:], bank[2][:, 8:16]))
            for half in range(2):
                q = slice(NQ * half, NQ * half + NQ)
                ins = dve.scalar_tensor_tensor(sk_p[:, q], bank[2][:, q], sk_flat[:, half:half + 1], sk_a[:, q],
                                               ALU.add, ALU.mult)
            ins.then_inc(s_skp, 1)
            key_part(1)
            dve.wait_ge(s_skT, 1)
            dve.tensor_copy(sk_pT[:], bank[2][0:8, 0:P]).then_inc(s_skTsb, 1)
            link(dve.tensor_tensor(gb_sum[:], vec[:, C_GB:C_GB + EXPERTS], vec[:, C_GB + EXPERTS:C_SC], ALU.add))
            rows_a(0)
            key_part(2)
            rows_b(0)
            key_part(3)
            rows_c(0)

            def low(k, e):
                low_part(dve, k, e).then_inc(s_lo_d, 1)

            choose_a(0)
            choose_b(0)
            low(0, 3)
            rows_a(1)
            low(0, 5)
            rows_b(1)
            for k in range(TRIOS):
                if k in (1, 3):
                    choose_a((k + 1) // 2)
                combine(TRIO * k)
                if k + 1 < TRIOS:
                    low(k + 1, 3)
                if k in (0, 2):
                    rows_c(k // 2 + 1)
                if k == 1:
                    rows_a(2)
                combine(TRIO * k + 1)
                if k + 1 < TRIOS:
                    low(k + 1, 5)
                if k in (1, 3):
                    choose_b((k + 1) // 2)
                combine(TRIO * k + 2)
                if k == 1:
                    rows_b(2)

        @block.tensor
        def _(pe_):
            mm = pe_.matmul

            pe_.wait_ge(s_ident, 1)
            pe_.wait_ge(s_ids, 1)
            for s in range(SEQS):
                ins = pe_.transpose(bank[0].bitcast(BF16)[:, ROWS * s:ROWS * s + ROWS], ids_b[:, s, :],
                                    ident_b[0:ROWS, 0:ROWS])
            ins.then_inc(s_idT, 1)
            pe_.wait_ge(s_hl, 1)
            pe_.wait_ge(s_ident, 2)
            for i in range(3):
                ins = pe_.transpose(bank[2][0:D, P * i:P * i + P], vy[:, i, :], ident[:])
            ins.then_inc(s_hT, 1)
            pe_.wait_ge(s_hTsb, 1)
            for i in range(3):
                mm(bank[3 + i][0:D, 0:3 * P], qkv_sb[:, D * i:D * i + D], hvT[:], start=True, stop=True).then_inc(s_qkv, 1)
            pe_.wait_ge(s_onej, 2)
            pe_.wait_ge(s_const, 2)
            for s in range(SEQS):
                for c in range(2):
                    for j in range(NQ):
                        mm(bank[1][:, 2 * s + c:2 * s + c + 1], oneh_j[:, JBLK * s + NQ * c + j, :], ones_h[:],
                           start=(j == 0), stop=(j == NQ - 1))
            mm(bank[1][:, 8:8 + ROWS], ones_b[:], skip_j[:], start=True, stop=True).then_inc(s_cnt, 1)
            pe_.wait_ge(s_qsb, 2)
            for i in range(3):
                ins = mm(bank[2][:, D * i:D * i + D], vT[:, P * i:P * i + P], qkv_sb[0:D, C_PROJ:C_PROJ + D], start=True, stop=True)
            ins.then_inc(s_vproj, 1)
            pe_.wait_ge(s_ksb, 1)
            pe_.wait_ge(s_absent, 1)
            for i, (a, b, k0) in enumerate(((S0, S1, 0), (S1, SK, P), (SK, GW, P))):
                mm(bank[6][:, a:b], qT[:, P * i:P * i + P], kT[:, k0:k0 + b - a], start=True, stop=False)
                ins = mm(bank[6][:, a:b], ones_b[:], absent_d[:, k0:k0 + b - a], start=False, stop=True)
            ins.then_inc(s_g, 1)

            def weights(t):
                s, half = tile_s(t)
                if t == 1:
                    pe_.wait_ge(s_idcol, 1)
                if t == 2:
                    pe_.wait_ge(s_cntread, 1)
                if t == 3:
                    pe_.wait_ge(s_skTsb, 1)
                js = (NQ, 2 * NQ)[half]
                for j in range(js):
                    z = TOE_FLAT + HALF * half - P * j
                    for part, toe in enumerate((toe_hi, toe_lo)):
                        ins = mm(bank[M_BANK[t]][:, :], oneh_j[:, JBLK * s + j, :], toe[:, z:z + HALF],
                                 start=(j == 0 and part == 0), stop=(j == js - 1 and part == 1))
                ins.then_inc(s_m, 1)

            def scores(t):
                s, half = tile_s(t)
                if t == 0:
                    pe_.wait_ge(s_qsb, 2)
                if t >= 2:
                    pe_.wait_ge(s_asb, t - 1)
                q0 = LEN * s + FIRST + HALF * half
                dst = bank[A_BANK[t % 2]][:, :]
                mm(dst, eg_hi[:, P * s:P * s + P], oneh_t[:, q0:q0 + HALF], start=True, stop=False)
                ins = mm(dst, eg_lo[:, P * s:P * s + P], oneh_t[:, q0:q0 + HALF], start=False, stop=(s == 0))
                if s:
                    for part, e in enumerate((eg_hi, eg_lo)):
                        ins = mm(dst, e[0:1, SK:SK + P], skip_row[:, q0 - LEN:q0 - LEN + HALF], start=False, stop=part == 1)
                ins.then_inc(s_a, 1)

            pe_.wait_ge(s_toe, 1)
            weights(0)
            weights(1)
            pe_.wait_ge(s_eg, 3)
            for s in range(SEQS):
                pe_.transpose(bank[3][:, P * s:P * s + P], eg[:, P * s:P * s + P], ident[:])
            pe_.transpose(bank[3][0:1, 2 * P:3 * P], eg[:, SK - 1:SK], ident[:]).then_inc(s_egT, 1)
            pe_.wait_ge(s_egs, 1)
            pe_.wait_ge(s_onet, 1)
            pe_.wait_ge(s_skrow, 1)
            scores(0)
            scores(1)
            pe_.wait_ge(s_vp, 1)
            for i in range(2 * NQ):
                js = NQ if i < NQ else 2 * NQ
                for j in range(js):
                    z = TOE_FLAT + P * (i - j)
                    for part, toe in enumerate((toe_hi, toe_lo)):
                        mm(bank[2][:, i:i + 1], toe[:, z:z + P], skip_j[:, j:j + 1],
                           start=(j == 0 and part == 0), stop=(j == js - 1 and part == 1))
            for i in range(2 * NQ):
                q0 = FIRST + P * i
                for part, e in enumerate((eg_hi, eg_lo)):
                    mm(bank[2][:, 8 + i:9 + i], oneh_t[:, LEN + q0:LEN + q0 + P], e[:, SK - 1:SK],
                       start=part == 0, stop=False)
                for part, e in enumerate((eg_hi, eg_lo)):
                    ins = mm(bank[2][:, 8 + i:9 + i], skip_row[:, q0:q0 + P], e[0:1, GW - 1:GW],
                             start=False, stop=part == 1)
            ins.then_inc(s_sk, 1)

            def result(b, i):
                u = bank[3][:, (D + 1) * i:(D + 1) * (i + 1)]
                h = bank[4][:, D * i:D * (i + 1)]
                if b < 2:
                    s = 1 - b
                    mm(u, egT[:, s, :], vh[:, s, :], start=True, stop=(s == 0))
                    if s:
                        mm(u, egT[0:1, 2, :], vh_skip[:], start=False, stop=True)
                    for part in range(3):
                        ins = mm(h, ident_h[:], h_part[:, part, s, :], start=part == 0, stop=part == 2)
                    return ins
                s, r = int(b < 10), (b - 2) % 8
                q0 = FIRST + P * r
                t = 2 * (1 - s) + r // NQ
                pe_.wait_ge(s_p, t + 1)
                mm(u, pT[:, t, P * (r % NQ):P * (r % NQ) + P], vp[:, s, :], start=True, stop=(s == 0))
                if s:
                    mm(u, sk_pT[:], v_sel[:, r, :], start=False, stop=True)
                for part in range(3):
                    ins = mm(h, oneh_t[:, LEN * s + q0:LEN * s + q0 + P], h_part[:, part, s, :],
                             start=part == 0, stop=(s == 0 and part == 2))
                if s:
                    for part in range(3):
                        ins = mm(h, skip_row[:, q0:q0 + P], h_part[0:1, part, 2, :], start=False, stop=part == 2)
                return ins

            def results(g):
                if g >= 1:
                    pe_.wait_ge(s_h2, g)
                for i in range(SIX):
                    ins = result(SIX * g + i, i)
                ins.then_inc(s_u, 1)

            def turn(g):
                pe_.wait_ge(s_xs, g + 1)
                if g == 0:
                    pe_.wait_ge(s_asb, 3)
                else:
                    pe_.wait_ge(s_lgread, g)
                for b in range(SIX):
                    ins = pe_.transpose(bank5h[:, P * b:P * b + P], xs[:, g % 2, b, :, :].rearrange("p a d -> p (a d)"),
                                        ident_h[:])
                ins.then_inc(s_xT, 1)

            def gate(g):
                pe_.wait_ge(s_xTsb, g + 1)
                for b in range(SIX):
                    for part, w in enumerate((w1_hi, w1_lo)):
                        ins = mm(LOGITS[:, EXPERTS * b:EXPERTS * (b + 1)], xT[:, g % 2, P * b:P * b + P],
                                 w[:, EXPERTS * HID:W1W], start=part == 0, stop=part == 1)
                ins.then_inc(s_lg, 1)

            def first_layer(k, e):
                n = EXPERTS * k + e
                if n >= 3:
                    pe_.wait_ge(s_hid, n - 2)
                for part, w in enumerate((w1_hi, w1_lo)):
                    ins = mm(bank[n % 3][:, 0:TRIO * P], w[:, HID * e:HID * (e + 1)],
                             xT[:, k // 2 % 2, TRIO * P * (k % 2):TRIO * P * (k % 2 + 1)], start=part == 0, stop=part == 1)
                ins.then_inc(s_z, 1)

            def second_layer(n):
                k, i = n // TRIO, n % TRIO
                y = bank[Y_BANK[n % 2]]
                pe_.wait_ge(s_hid, EXPERTS * (k + 1))
                if n >= 2:
                    pe_.wait_ge(s_prod, n - 1)
                mm(y[:, :], ones_b[0:3, :], b2_k[:], start=True, stop=True)
                for e in range(EXPERTS):
                    for w in (w2_hi, w2_lo):
                        mm(y[:, D * e:D * e + D], hid_hi[:, k % 2, e, P * i:P * i + P], w[:, D * e:D * e + D],
                           start=False, stop=False, skip_group_check=True)
                if i == 0:
                    wait_lo(pe_, EXPERTS * k + LO_DVE[-1])
                    wait_lo(pe_, EXPERTS * k + LO_POOL[-1])
                for e in range(EXPERTS):
                    ins = mm(y[:, D * e:D * e + D], hid_lo[:, k % 2, e, P * i:P * i + P], w2_hi[:, D * e:D * e + D],
                             start=False, stop=True, skip_group_check=True)
                ins.then_inc(s_y, 1)

            def look(dst, s, col, n, q):
                for part in range(3):
                    ins = mm(dst, oneh_t[:, col:col + n], fin_part[:, part, 1 - s, :], start=part == 0,
                             stop=(s == 0 and part == 2))
                if s:
                    for part in range(3):
                        ins = mm(dst, skip_row[:, q:q + n], fin_part[0:1, part, 2, :], start=False, stop=part == 2)
                return ins

            def look_up(n):
                if n == 0:
                    pe_.wait_ge(s_fpart, 1)
                    pe_.wait_ge(s_lgread, 3)
                else:
                    pe_.wait_ge(s_looked, n)
                if n < 2:
                    for i in range(FIRST // P):
                        ins = look(bank[5][:, D * i:D * i + D], n, LEN * n + P * i, P, P * i)
                else:
                    ins = look(bank[5][0:1, 0:D], 1, SEQS * LEN, 1, LEN)
                ins.then_inc(s_look, 1)

            pe_.wait_ge(s_hb, 1)
            pe_.wait_ge(s_skp, 1)
            pe_.transpose(bank[2][0:8, 0:P], sk_p[:], ident[:]).then_inc(s_skT, 1)
            pe_.wait_ge(s_vh, 1)
            pe_.wait_ge(s_egTsb, 1)
            pe_.wait_ge(s_skTsb, 1)
            results(0)
            weights(2)
            scores(2)
            weights(3)
            scores(3)
            pe_.wait_ge(s_w1s, 1)
            turn(0)
            pe_.wait_ge(s_xTsb, 1)
            pe_.wait_ge(s_w2s, 1)
            pe_.wait_ge(s_p, 4)
            first_layer(0, 0)
            gate(0)
            for e in range(1, EXPERTS):
                first_layer(0, e)
                if e == 3:
                    results(1)
            pe_.wait_ge(s_asb, 4)
            pe_.wait_ge(loads["b2_k"], 16)
            for k in range(TRIOS):
                if k + 1 < TRIOS:
                    if (k + 1) % 2 == 0:
                        turn((k + 1) // 2)
                        pe_.wait_ge(s_xTsb, (k + 1) // 2 + 1)
                    for e in range(2):
                        first_layer(k + 1, e)
                    if (k + 1) % 2 == 0:
                        gate((k + 1) // 2)
                for i in range(TRIO):
                    second_layer(TRIO * k + i)
                    if k + 1 < TRIOS:
                        for e in range(2 + 2 * i, 4 + 2 * i):
                            first_layer(k + 1, e)
                        if k == 1 and i == 0:
                            results(2)
                        if k == 4:
                            look_up(i)


def kernel(**inputs):
    import numpy as _np
    import concourse.bacc as _bacc
    from concourse import mybir as _mybir
    from concourse.bass_utils import run_bass_kernel_spmd as _run

    a = {n.removeprefix("L0_"): _np.asarray(v) for n, v in inputs.items()}
    table = a["attn_bias_table"]
    w1 = a["ffn_W1"].transpose(1, 0, 2).reshape(D, -1)
    w1 = _np.concatenate([w1, a["ffn_Wg"]], 1)
    proj = _np.concatenate([a["attn_proj_w"], a["attn_ln1_g"][:, None], a["attn_ln1_b"][:, None]], 1)
    proj = _np.concatenate([proj, proj[:1]], 0)
    packed = {
        "x": a["x"],
        "token_w": a["tok_token_W"],
        "vecs": _np.concatenate([a["tok_pe"][0], a["tok_pe"][1], a["tok_token_W"][PAD_ID], a["attn_ln2_g"],
                                 a["attn_ln2_b"], a["attn_proj_b"], a["ffn_bg"], a["ffn_bias"],
                                 a["attn_scale"].reshape(1)]),
        "qkv": _np.concatenate([_np.concatenate([a["attn_qkv_w"], a["attn_qkv_b"][None]], 0), proj], 1),
        "bias_table": _np.concatenate([table, _np.repeat(table[-1:], 1151 - TABLE)]),
        "w1g": _np.concatenate([w1, w1], 0),
        "w2b1": _np.concatenate([a["ffn_W2"].transpose(1, 0, 2).reshape(HID, -1), a["ffn_b1"].T], 1),
        "b2": a["ffn_b2"].reshape(1, -1),
    }
    nc = _bacc.Bacc("TRN2", target_bir_lowering=False, num_devices=1)
    arrays, args = {}, []
    for name, v in packed.items():
        v = _np.ascontiguousarray(v)
        arrays[f"in_{name}_dram"] = v
        args.append(nc.dram_tensor(f"in_{name}_dram", v.shape, _mybir.dt.from_np(v.dtype), kind="ExternalInput").ap())
    args.append(nc.dram_tensor("out_0_dram", (SEQS, LEN, D), F32, kind="ExternalOutput").ap())
    build(nc, *args)
    r = _run(nc, [arrays], core_ids=[0])
    return r.results[0]["out_0_dram"]
```

```python
from contextlib import ExitStack

import concourse.bass as bass
from concourse import mybir

F32 = mybir.dt.float32
F16 = mybir.dt.float16
BF16 = mybir.dt.bfloat16
I32 = mybir.dt.int32
U32 = mybir.dt.uint32
ALU = mybir.AluOpType
ACT = mybir.ActivationFunctionType
AX = mybir.AxisListType

P = 128
VOCAB = 128
D = 64
SEQS, LEN = 2, 2048
ROWS = LEN // P
TABLE = 1023
FIRST = LEN // 2
SEP_ID, PAD_ID = 13, 1
SKIP_ID = 128
EXPERTS, HID = 8, 128
EPS = 1e-5
ABSENT = -1e30
ESCALE = 32768.0
XSCALE = 64.0
HSCALE = 32.0
YSCALE = HSCALE * XSCALE
TOE = 1408
TOE_FLAT = TOE - 1024
NQ = 4
HALF = NQ * P
JBLK = FIRST // P
FIRST_BLOCK = (0, 2, 6, 10, 14)
SIZE = (2, 4, 4, 4, 4)
UNITS = len(SIZE)
BLOCKS = sum(SIZE)
MAXB = max(SIZE)
BY_POOL = 3
HSLOTS = 6
S0, S1, SK = 0, 128, 257
GW = 386
IDS = 257
W1W = EXPERTS * HID + EXPERTS
C_G2, C_B2, C_PB, C_GB, C_SC = 3 * D, 4 * D, 5 * D, 6 * D, 6 * D + 2 * EXPERTS
VECS = C_SC + 1
C_PROJ, C_G1, C_B1 = 3 * D, 4 * D, 4 * D + 1
QW = 4 * D + 2


def build(nc, x, token_w, vecs, qkv, bias_table, w1g, w2b1, b2, out):
    ids_dram = nc.dram_tensor("ids_scratch", (SEQS, LEN), BF16, kind="Internal").ap()

    with ExitStack() as ctx:
        def sb(name, shape, dt=F32):
            return ctx.enter_context(nc.sbuf_tensor(name, shape, dt))

        def sem(name):
            return ctx.enter_context(nc.semaphore(name))

        bank = [ctx.enter_context(nc.psum_tensor(f"bank{i}", [P, 512], F32)) for i in range(8)]

        iota_row = sb("iota_row", [P, P])
        iota_h = sb("iota_h", [P, P], F16)
        iota_p = sb("iota_p", [P, 1])
        ident = sb("ident", [P, P])
        ident_h = sb("ident_h", [P, P], F16)
        ident_b = sb("ident_b", [P, P], BF16)
        ones_h = sb("ones_h", [P, 1], F16)
        ones_b = sb("ones_b", [P, P], BF16)
        neghalf = sb("neghalf", [P, 8])
        ids_i = sb("ids_i", [ROWS, SEQS, P], I32)
        ids_f = sb("ids_f", [ROWS, SEQS, P])
        is_sep = sb("is_sep", [ROWS, P])
        is_pad = sb("is_pad", [ROWS, P])
        ids_b = sb("ids_b", [ROWS, SEQS, P], BF16)
        id_col = sb("id_col", [P, SEQS * ROWS])
        oneh_j = sb("oneh_j", [P, SEQS * JBLK, P], F16)
        skip_j = sb("skip_j", [P, ROWS], F16)
        ids_all = sb("ids_all", [P, SEQS * LEN + 1], BF16)
        oneh_t = sb("oneh_t", [P, SEQS * LEN + 1], F16)
        oneh_junk = sb("oneh_junk", [P, LEN + 1], F16)
        skip_row = sb("skip_row", [1, LEN + 1], F16)
        table_all = sb("table_all", [P, TABLE])
        hankel = sb("hankel", [P, 1024])
        tmax = sb("tmax", [P, 2])
        nbmax = sb("nbmax", [P, 1])
        toe_hi = sb("toe_hi", [P, TOE], F16)
        toe_lo = sb("toe_lo", [P, TOE], F16)
        flat = sb("flat", [P, 1])
        w_tok = sb("w_tok", [P, D])
        vec = sb("vec", [P, VECS])
        hv = vec[:, 0:3 * D].rearrange("p (s d) -> p s d", d=D)
        qkv_sb = sb("qkv_sb", [D + 1, QW])
        gb_sum = sb("gb_sum", [P, EXPERTS])
        w1_sb = sb("w1_sb", [P, W1W])
        w1_hi = sb("w1_hi", [P, W1W], F16)
        w1_lo = sb("w1_lo", [P, W1W], F16)
        w2_sb = sb("w2_sb", [P, EXPERTS * D + EXPERTS])
        w2_hi = sb("w2_hi", [P, EXPERTS * D], F16)
        w2_lo = sb("w2_lo", [P, EXPERTS * D], F16)
        b1_col = sb("b1_col", [P, EXPERTS])
        b2_row = sb("b2_row", [1, EXPERTS * D])
        b2_rest = sb("b2_rest", [1, EXPERTS * D])
        b2_part = sb("b2_part", [1, 3, EXPERTS * D], BF16)
        b2_k = sb("b2_k", [3, EXPERTS * D], BF16)
        pmask = sb("pmask", [P, 1])
        hb = sb("hb", [P, 3, D])
        h_part = sb("h_part", [P, 3, 3, D], BF16)
        vy = sb("vy", [P, 3, D])
        vstat = sb("vstat", [P, 3, 6])
        vmv = sb("vmv", [P, 3, 2])
        vvar = sb("vvar", [P, 3])
        vrs = sb("vrs", [P, 3])
        hvT = sb("hvT", [D + 1, IDS])
        qT = sb("qT", [D, IDS])
        kT = sb("kT", [D, IDS])
        vT = sb("vT", [D, IDS])
        vp = sb("vp", [P, 3, D + 1])
        vsum = sb("vsum", [P, 3])
        vmean = sb("vmean", [P, 3])
        vh = sb("vh", [P, SEQS, D + 1])
        vh_skip = sb("vh_skip", [1, D + 1])
        v_sel = sb("v_sel", [8, 8, D + 1])
        cnt_late = sb("cnt_late", [P, SEQS])
        cnt = sb("cnt", [P, SEQS, 2])
        cnt_half = sb("cnt_half", [P, SEQS, 3])
        skc = sb("skc", [P, ROWS])
        sk_half = sb("sk_half", [P, 3])
        flat_w = sb("flat_w", [P, SEQS, 2])
        sk_flat = sb("sk_flat", [P, 2])
        absent = sb("absent", [P, 3])
        absent_d = sb("absent_d", [P, IDS], BF16)
        gmax = sb("gmax", [P, 3])
        eg = sb("eg", [P, GW])
        eg_hi = sb("eg_hi", [P, GW], F16)
        eg_lo = sb("eg_lo", [P, GW], F16)
        egT = sb("egT", [P, 3, P])
        a_sb = sb("a_sb", [P, 2, HALF])
        pT = sb("pT", [P, 4, HALF])
        sk_a = sb("sk_a", [P, 8])
        sk_p = sb("sk_p", [P, 8])
        sk_pT = sb("sk_pT", [8, P])
        h_all = sb("h_all", [P, BLOCKS, D])
        fin_all = sb("fin_all", [P, BLOCKS, D])
        usq = sb("usq", [P, MAXB, D + 1])
        uss = sb("uss", [P, MAXB])
        deps = sb("deps", [P, MAXB])
        var1 = sb("var1", [P, MAXB])
        rs1 = sb("rs1", [P, MAXB])
        on = sb("on", [P, MAXB, D])
        og = sb("og", [P, MAXB, D])
        stat = sb("stat", [P, MAXB, 6])
        mv = sb("mv", [P, MAXB, 2])
        var2 = sb("var2", [P, MAXB])
        rs2 = sb("rs2", [P, MAXB])
        xc = sb("xc", [P, MAXB, D])
        xn = sb("xn", [P, MAXB, D])
        xs = sb("xs", [P, 2, MAXB, 2, D], F16)
        xT = sb("xT", [P, 2, MAXB * P], F16)
        lg = sb("lg", [P, MAXB, EXPERTS])
        top = sb("top", [P, MAXB, 8])
        tix = sb("tix", [P, MAXB, 8], U32)
        tixf = sb("tixf", [P, 2, MAXB])
        gd = sb("gd", [P, MAXB])
        ge = sb("ge", [P, MAXB])
        gs = sb("gs", [P, MAXB])
        gw = sb("gw", [P, 2, MAXB])
        sel = sb("sel", [P, 2, MAXB, EXPERTS])
        comb = sb("comb", [P, 2, MAXB, EXPERTS])
        hid = sb("hid", [P, HSLOTS, MAXB * P])
        hid_hi = sb("hid_hi", [P, 2, EXPERTS, MAXB * P], F16)
        hid_lo = sb("hid_lo", [P, 2, EXPERTS, MAXB * P], F16)
        prod = sb("prod", [P, 2, EXPERTS, D])
        acc = sb("acc", [P, MAXB, D])
        fin_part = sb("fin_part", [P, 3, 3, D], BF16)
        looked = sb("looked", [P, SEQS, 8, D])
        looked1 = sb("looked1", [1, D])
        rest = sb("rest", [P, 3 * D])

        loads = {n: sem("ld_" + n) for n in (
            "ids", "table", "hankel", "scratch", "ids_all", "w_tok", "vecs", "qkv", "w1", "w2", "b2", "b2_k")}
        s_const = sem("s_const")
        s_dve = sem("s_dve")
        s_pool = sem("s_pool")
        s_ident = sem("s_ident")
        s_ids = sem("s_ids")
        s_idT = sem("s_idT")
        s_idcol = sem("s_idcol")
        s_onej = sem("s_onej")
        s_onejp = sem("s_onejp")
        s_cnt = sem("s_cnt")
        s_cntread = sem("s_cntread")
        s_cntlate = sem("s_cntlate")
        s_absent = sem("s_absent")
        s_onet = sem("s_onet")
        s_skrow = sem("s_skrow")
        s_nbmax = sem("s_nbmax")
        s_expb = sem("s_expb")
        s_toe = sem("s_toe")
        s_hv = sem("s_hv")
        s_vvar = sem("s_vvar")
        s_vrs = sem("s_vrs")
        s_hl = sem("s_hl")
        s_hT = sem("s_hT")
        s_hTsb = sem("s_hTsb")
        s_qkv = sem("s_qkv")
        s_qsb = sem("s_qsb")
        s_ksb = sem("s_ksb")
        s_vproj = sem("s_vproj")
        s_vp = sem("s_vp")
        s_g = sem("s_g")
        s_gmax = sem("s_gmax")
        s_eg = sem("s_eg")
        s_egs = sem("s_egs")
        s_egT = sem("s_egT")
        s_egTsb = sem("s_egTsb")
        s_vh = sem("s_vh")
        s_hb = sem("s_hb")
        s_w1s = sem("s_w1s")
        s_b2p = sem("s_b2p")
        s_m = sem("s_m")
        s_a = sem("s_a")
        s_asb = sem("s_asb")
        s_p = sem("s_p")
        s_sk = sem("s_sk")
        s_skp = sem("s_skp")
        s_skT = sem("s_skT")
        s_skTsb = sem("s_skTsb")
        s_u = sem("s_u")
        s_usq = sem("s_usq")
        s_var1 = sem("s_var1")
        s_rs1 = sem("s_rs1")
        s_h2 = sem("s_h2")
        s_var2 = sem("s_var2")
        s_rs2 = sem("s_rs2")
        s_xs = sem("s_xs")
        s_xT = sem("s_xT")
        s_xTsb = sem("s_xTsb")
        s_lg = sem("s_lg")
        s_lgread = sem("s_lgread")
        s_gd = sem("s_gd")
        s_ge = sem("s_ge")
        s_z = sem("s_z")
        s_hid = sem("s_hid")
        s_lo_d = sem("s_lo_d")
        s_lo_p = sem("s_lo_p")
        s_w2s = sem("s_w2s")
        s_y = sem("s_y")
        s_prod = sem("s_prod")
        s_fin = sem("s_fin")
        s_fpart = sem("s_fpart")
        s_look = sem("s_look")
        s_looked = sem("s_looked")
        s_out = sem("s_out")

        def bcast(ap, shape, axis):
            return ap.unsqueeze(axis).to_broadcast(shape)

        def unit_of(n):
            u = max(u for u in range(UNITS) if FIRST_BLOCK[u] <= n)
            return u, n - FIRST_BLOCK[u]

        def tile_s(t):
            return 1 - t // 2, t % 2

        LO_DVE = ((), (), (), (), (3, 5))
        LO_POOL = tuple(tuple(e for e in range(EXPERTS) if e not in on_dve) for on_dve in LO_DVE)

        def wait_lo(eng, n):
            k, e = n // EXPERTS, n % EXPERTS
            s, by = (s_lo_d, LO_DVE) if e in LO_DVE[k] else (s_lo_p, LO_POOL)
            eng.wait_ge(s, sum(len(by[i]) for i in range(k)) + by[k].index(e) + 1)

        def low_part(eng, k, e):
            n = EXPERTS * k + e
            eng.wait_ge(s_hid, n + 1)
            if k >= 2:
                eng.wait_ge(s_y, FIRST_BLOCK[k - 1])
            m = P * SIZE[k]
            return eng.tensor_tensor(hid_lo[:, k % 2, e, 0:m], hid[:, n % HSLOTS, 0:m], hid_hi[:, k % 2, e, 0:m], ALU.subtract)

        M_BANK = [7, 2, 2, 2]
        A_BANK = [5, 5, 5, 5]
        Y_BANK = [6, 7]
        bank5h = bank[5].bitcast(F16)
        LOGITS = bank[5][:, 448:448 + MAXB * EXPERTS]

        class Chain:

            def __init__(self, eng, s):
                self.eng, self.s, self.n = eng, s, 0

            def link(self, ins):
                self.n += 1
                ins.then_inc(self.s, 1)
                self.eng.wait_ge(self.s, self.n)

        block = ctx.enter_context(nc.Block())

        @block.sync
        def _(sp):
            sp.dma_start(ids_i[:], x.rearrange("s (r p) -> r s p", p=P)).then_inc(loads["ids"], 16)
            sp.dma_start(vec[:], vecs.partition_broadcast(P)).then_inc(loads["vecs"], 16)
            sp.dma_start(table_all[:], bias_table[0:TABLE].partition_broadcast(P)).then_inc(loads["table"], 16)
            sp.wait_ge(s_ids, 1)
            sp.dma_start(ids_dram.rearrange("s (r p) -> r s p", p=P), ids_b[:]).then_inc(loads["scratch"], 16)
            sp.dma_start(hankel[:], bass.AP(bias_table.tensor, 0, [[1, P], [1, 1024]])).then_inc(loads["hankel"], 16)
            sp.wait_ge(loads["scratch"], 16)
            sp.dma_start(ids_all[:, 0:SEQS * LEN],
                         ids_dram.rearrange("s n -> (s n)").partition_broadcast(P)).then_inc(loads["ids_all"], 16)
            sp.dma_start(w1_sb[:], w1g).then_inc(loads["w1"], 16)
            sp.dma_start(b2_row[:], b2).then_inc(loads["b2"], 16)
            sp.dma_start(w2_sb[:], w2b1).then_inc(loads["w2"], 16)
            sp.wait_ge(s_b2p, 1)
            sp.dma_start(b2_k[:], b2_part[:]).then_inc(loads["b2_k"], 16)
            stores = 0

            def store(dst, src):
                sp.dma_start(dst, src).then_inc(s_out, 16)

            def rows_of(s, b, n):
                r0 = FIRST + P * (b - (2 if s else 10))
                return out[s, r0:r0 + P * n, :].rearrange("(b p) d -> p b d", p=P)

            for u in range(1, UNITS):
                sp.wait_ge(s_fin, u + 1)
                b, n = FIRST_BLOCK[u], SIZE[u]
                if u == 1:
                    store(out[1, FIRST + 1:FIRST + P, :], fin_all[1:P, b, :])
                    store(rows_of(1, b + 1, n - 1), fin_all[:, b + 1:b + n, :])
                    stores += 1
                else:
                    store(rows_of(int(b < 10), b, n), fin_all[:, b:b + n, :])
                stores += 1
                if u == 3:
                    for s in range(SEQS):
                        sp.wait_ge(s_looked, s + 1)
                        store(out[s, 0:FIRST, :].rearrange("(n p) d -> p n d", p=P), looked[:, s, :, :])
                    sp.wait_ge(s_looked, 3)
                    store(out[1, FIRST:FIRST + 1, :], looked1[:])
                    stores += 3
            sp.wait_ge(s_out, 16 * stores)

        @block.gpsimd
        def _(pool):
            ch = Chain(pool, s_pool)
            link = ch.link
            pool.iota(iota_row[:], [[1, P]], base=0, channel_multiplier=0,
                      allow_small_or_imprecise_dtypes=True)
            pool.iota(iota_p[:], [[0, 1]], base=0, channel_multiplier=1,
                      allow_small_or_imprecise_dtypes=True).then_inc(s_const, 1)
            pool.memset(neghalf[:], -0.5)
            pool.memset(vp[:], 1.0)
            pool.memset(ones_h[:], 1.0)
            pool.memset(ones_b[:], 1.0).then_inc(s_const, 1)
            pool.wait_ge(s_const, 2)
            for n in range(2):
                pool.wait_ge(s_vvar, n + 1)
                pool.tensor_tensor(vrs[:], vvar[:], neghalf[:, 0:3], ALU.pow).then_inc(s_vrs, 1)
            pool.wait_ge(s_idcol, 1)
            pool.wait_ge(s_ident, 1)
            for c in range(BY_POOL):
                pool.tensor_scalar(oneh_j[:, c, :], iota_h[:], id_col[:, c:c + 1], 0.0, ALU.is_equal, ALU.add).then_inc(s_onejp, 1)

            def parts(src, dst, left):
                link(pool.tensor_copy(dst(0), src))
                link(pool.tensor_tensor(left, src, dst(0), ALU.subtract))
                link(pool.tensor_copy(dst(1), left))
                link(pool.tensor_tensor(left, left, dst(1), ALU.subtract))
                return pool.tensor_copy(dst(2), left)

            rest3 = rest[:].rearrange("p (s d) -> p s d", d=D)
            pool.wait_ge(s_hv, 1)
            link(pool.tensor_tensor(hb[:], hv, bcast(vec[:, C_B2:C_B2 + D], [P, 3, D], 1), ALU.add))
            parts(hb[:], lambda i: h_part[:, i], rest3).then_inc(s_hb, 1)
            def w1_parts():
                pool.wait_ge(loads["w2"], 16)
                pool.tensor_scalar(b1_col[:], w2_sb[:, EXPERTS * D:], HSCALE, 0.0, ALU.mult, ALU.add)
                pool.wait_ge(loads["w1"], 16)
                link(pool.tensor_scalar(w1_sb[:], w1_sb[:], XSCALE, 0.0, ALU.mult, ALU.add))
                link(pool.tensor_copy(w1_hi[:], w1_sb[:]))
                pool.tensor_tensor(w1_lo[:], w1_sb[:], w1_hi[:], ALU.subtract).then_inc(s_w1s, 1)

            def table_values():
                pool.wait_ge(s_vp, 2)
                pool.wait_ge(s_absent, 1)
                for s in range(SEQS):
                    pool.tensor_scalar(vh[:, s, :], vp[:, s, :], cnt_half[:, s, 2:3], 0.0, ALU.mult, ALU.add)
                link(pool.tensor_scalar(vh_skip[:], vp[0:1, 2, :], sk_half[0:1, 2:3], 0.0, ALU.mult, ALU.add))
                pool.tensor_tensor(v_sel[:], ident[0:8, 0:8].unsqueeze(2).to_broadcast([8, 8, D + 1]),
                                   bcast(vp[0:8, 2, :], [8, 8, D + 1], 1), ALU.mult).then_inc(s_vh, 1)

            def w2_parts():
                pool.wait_ge(loads["w2"], 16)
                w2 = w2_sb[:, 0:EXPERTS * D]
                link(pool.tensor_scalar(w2, w2, XSCALE, 0.0, ALU.mult, ALU.add))
                link(pool.tensor_copy(w2_hi[:], w2))
                pool.tensor_tensor(w2_lo[:], w2, w2_hi[:], ALU.subtract).then_inc(s_w2s, 1)

            def rsqrt1(g):
                pool.wait_ge(s_var1, g + 1)
                pool.tensor_tensor(rs1[:, 0:SIZE[g]], var1[:, 0:SIZE[g]], neghalf[:, 0:SIZE[g]], ALU.pow).then_inc(s_rs1, 1)

            def rsqrt2(g):
                pool.wait_ge(s_var2, g + 1)
                pool.tensor_tensor(rs2[:, 0:SIZE[g]], var2[:, 0:SIZE[g]], neghalf[:, 0:SIZE[g]], ALU.pow).then_inc(s_rs2, 1)

            def fin_parts(step):
                src = fin_all[:, 0:3, :]
                if step == 0:
                    pool.wait_ge(s_fin, 2)
                    link(pool.tensor_copy(fin_part[:, 0], src))
                elif step == 1:
                    link(pool.tensor_tensor(rest3, src, fin_part[:, 0], ALU.subtract))
                elif step == 2:
                    link(pool.tensor_copy(fin_part[:, 1], rest3))
                elif step == 3:
                    link(pool.tensor_tensor(rest3, rest3, fin_part[:, 1], ALU.subtract))
                else:
                    pool.tensor_copy(fin_part[:, 2], rest3).then_inc(s_fpart, 1)


            def low(k, e):
                low_part(pool, k, e).then_inc(s_lo_p, 1)

            w1_parts(); table_values(); rsqrt1(0); rsqrt2(0); w2_parts(); rsqrt1(1); low(0, 0)
            low(0, 1); low(0, 2); rsqrt2(1); low(0, 3); low(0, 4); low(0, 5); rsqrt1(2); low(0, 6)
            low(0, 7); low(1, 0); low(1, 1); rsqrt2(2); low(1, 2); low(1, 3); low(1, 4); low(1, 5)
            rsqrt1(3); low(1, 6); low(1, 7); low(2, 0); low(2, 1); low(2, 2); low(2, 3); low(2, 4)
            rsqrt2(3); low(2, 5); low(2, 6); low(2, 7); fin_parts(0); fin_parts(1); fin_parts(2)
            fin_parts(3); rsqrt1(4); low(3, 0); low(3, 1); fin_parts(4); rsqrt2(4); low(3, 2); low(3, 3)
            low(3, 4); low(3, 5); low(3, 6); low(3, 7); low(4, 0); low(4, 1); low(4, 2); low(4, 4)
            low(4, 6); low(4, 7)

        @block.scalar
        def _(act):
            act.dma_start(w_tok[:], token_w).then_inc(loads["w_tok"], 16)
            act.dma_start(qkv_sb[:], qkv).then_inc(loads["qkv"], 16)
            act.preload_act_table(ACT.Exp)
            act.wait_ge(s_hT, 1)
            act.wait_ge(loads["qkv"], 16)
            act.activation(hvT[0:D, :], bank[2][0:D, 0:IDS], ACT.Identity, bias=qkv_sb[0:D, C_B1:C_B1 + 1],
                           scale=qkv_sb[0:D, C_G1:C_G1 + 1]).then_inc(s_hTsb, 1)
            act.wait_ge(loads["hankel"], 16)
            act.wait_ge(s_nbmax, 1)
            act.activation(hankel[:], hankel[:], ACT.Exp, bias=nbmax[:, 0:1]).then_inc(s_expb, 1)
            act.wait_ge(s_qkv, 1)
            act.copy(qT[:], bank[3][0:D, 0:IDS]).then_inc(s_qsb, 1)

            def count_late(s):
                act.wait_ge(s_onet, s + 1)
                act.activation(oneh_junk[:, FIRST * s:FIRST * (s + 1) + s], oneh_t[:, LEN * s + FIRST:LEN * (s + 1) + s],
                               ACT.Copy, accum_out=cnt_late[:, s:s + 1]).then_inc(s_cntlate, 1)

            def read_v():
                act.wait_ge(s_qkv, 3)
                act.copy(vT[:], bank[5][0:D, 0:IDS]).then_inc(s_qsb, 1)

            def pair_exps():
                act.wait_ge(s_gmax, 1)
                for n, (a, b) in enumerate(((S0, S1), (S1, SK), (SK, GW))):
                    act.activation(eg[:, a:b], bank[6][:, a:b], ACT.Exp, bias=gmax[:, n:n + 1]).then_inc(s_eg, 1)

            def read_turned_exps():
                act.wait_ge(s_egT, 1)
                act.copy(egT[:, 0:2, :], bank[3][:, 0:2 * P].rearrange("p (s d) -> p s d", d=P))
                act.copy(egT[0:1, 2, :], bank[3][0:1, 2 * P:3 * P]).then_inc(s_egTsb, 1)

            def squares(g):
                act.wait_ge(s_u, g + 1)
                if g >= 1:
                    act.wait_ge(s_var1, g)
                act.activation(usq[:, 0:SIZE[g], :], bank[3][:, 0:SIZE[g] * (D + 1)].rearrange("p (b d) -> p b d", d=D + 1),
                               ACT.Square).then_inc(s_usq, 1)

            def score_tile(t):
                act.wait_ge(s_a, t + 1)
                if t >= 2:
                    act.wait_ge(s_p, t - 1)
                act.copy(a_sb[:, t % 2, :], bank[A_BANK[t]][:, :]).then_inc(s_asb, 1)

            def read_turned(g):
                act.wait_ge(s_xT, g + 1)
                if g >= 2:
                    act.wait_ge(s_z, EXPERTS * (g - 1))
                act.copy(xT[:, g % 2, 0:P * SIZE[g]], bank5h[:, 0:P * SIZE[g]]).then_inc(s_xTsb, 1)

            def hidden(k, e):
                n = EXPERTS * k + e
                if n == 0:
                    act.wait_ge(s_w1s, 1)
                act.wait_ge(s_z, n + 1)
                if n >= HSLOTS:
                    wait_lo(act, n - HSLOTS)
                if k >= 2:
                    act.wait_ge(s_y, FIRST_BLOCK[k - 1])
                m = P * SIZE[k]
                both = (hid[:, n % HSLOTS, 0:m], hid_hi[:, k % 2, e, 0:m])
                for dst in both[:1 if e in LO_DVE[k] else 2]:
                    ins = act.activation(dst, bank[n % 2][:, 0:m], ACT.Relu, bias=b1_col[:, e:e + 1],
                                         scale=HSCALE / (XSCALE * XSCALE))
                ins.then_inc(s_hid, 1)

            def choice_exp(g):
                act.wait_ge(s_gd, g + 1)
                act.activation(ge[:, 0:SIZE[g]], gd[:, 0:SIZE[g]], ACT.Exp).then_inc(s_ge, 1)

            def read_look(n):
                act.wait_ge(s_look, n + 1)
                if n < 2:
                    act.copy(looked[:, n, :, :], bank[5][:, :].rearrange("p (n d) -> p n d", d=D)).then_inc(s_looked, 1)
                else:
                    act.copy(looked1[:], bank[5][0:1, 0:D]).then_inc(s_looked, 1)

            count_late(0); count_late(1); read_v(); pair_exps(); read_turned_exps(); squares(0)
            score_tile(0); read_turned(0); choice_exp(0); squares(1); hidden(0, 0); hidden(0, 1)
            hidden(0, 2); hidden(0, 3); score_tile(1); hidden(0, 4); hidden(0, 5); squares(2)
            read_turned(1); hidden(0, 6); hidden(0, 7); choice_exp(1); score_tile(2); hidden(1, 0)
            hidden(1, 1); hidden(1, 2); hidden(1, 3); hidden(1, 4); hidden(1, 5); squares(3)
            read_turned(2); hidden(1, 6); hidden(1, 7); hidden(2, 0); hidden(2, 1); choice_exp(2)
            hidden(2, 2); score_tile(3); hidden(2, 3); hidden(2, 4); hidden(2, 5); hidden(2, 6)
            hidden(2, 7); read_turned(3); squares(4); hidden(3, 0); hidden(3, 1); hidden(3, 2)
            choice_exp(3); hidden(3, 3); hidden(3, 4); hidden(3, 5); hidden(3, 6); read_turned(4)
            hidden(3, 7); hidden(4, 0); hidden(4, 1); hidden(4, 2); hidden(4, 3); hidden(4, 4)
            choice_exp(4); hidden(4, 5); hidden(4, 6); hidden(4, 7); read_look(0); read_look(1)
            read_look(2)

        @block.vector
        def _(dve):
            ch = Chain(dve, s_dve)
            link = ch.link

            dve.memset(hvT[D:D + 1, :], 1.0)
            dve.wait_ge(s_const, 1)
            dve.tensor_scalar(ident_b[:], iota_row[:], iota_p[:, 0:1], None, ALU.is_equal)
            dve.tensor_copy(iota_h[:], iota_row[:])
            dve.tensor_scalar(pmask[:], iota_p[:], 1.0, None, ALU.min).then_inc(s_ident, 1)
            dve.tensor_scalar(ident[:], iota_row[:], iota_p[:, 0:1], None, ALU.is_equal)
            dve.tensor_scalar(ident_h[:], iota_row[:], iota_p[:, 0:1], None, ALU.is_equal).then_inc(s_ident, 1)
            dve.wait_ge(loads["ids"], 16)
            link(dve.tensor_copy(ids_f[:], ids_i[:]))
            dve.tensor_scalar(is_sep[:], ids_f[:, 0, :], float(SEP_ID), float(SKIP_ID - PAD_ID), ALU.is_equal, ALU.mult)
            link(dve.tensor_scalar(is_pad[:], ids_f[:, 1, :], float(PAD_ID), None, ALU.is_equal))
            link(dve.tensor_tensor(is_pad[:], is_pad[:], is_sep[:], ALU.mult))
            dve.tensor_copy(ids_b[:, 0, :], ids_f[:, 0, :])
            dve.tensor_tensor(ids_b[:, 1, :], ids_f[:, 1, :], is_pad[:], ALU.add).then_inc(s_ids, 1)
            dve.wait_ge(s_ident, 1)
            dve.wait_ge(loads["w_tok"], 16)
            dve.wait_ge(loads["vecs"], 16)
            dve.scalar_tensor_tensor(hv[:, 0, :], w_tok[:], pmask[:, 0:1], hv[:, 0, :], ALU.mult, ALU.add)
            dve.scalar_tensor_tensor(hv[:, 1, :], w_tok[:], pmask[:, 0:1], hv[:, 1, :], ALU.mult, ALU.add).then_inc(s_hv, 1)
            dve.wait_ge(s_hv, 1)

            def row_stats(src, stats, means, var, n, mul, add, signal):
                for i in range(n):
                    ins = dve.bn_stats(stats[:, i, :], src[:, i, :])
                link(ins)
                for i in range(n):
                    ins = dve.bn_aggr(means[:, i, :], stats[:, i, :])
                link(ins)
                dve.tensor_scalar(var[:], means[:, :, 1], mul, add, ALU.mult, ALU.add).then_inc(signal, 1)

            def centre(dst, src, means, n):
                return dve.tensor_tensor(dst, src, means[:, :, 0].unsqueeze(2).to_broadcast([P, n, D]), ALU.subtract)

            def rescale(dst, src, rs, n):
                return dve.tensor_tensor(dst, src, rs[:].unsqueeze(2).to_broadcast([P, n, D]), ALU.mult)

            row_stats(hv, vstat, vmv, vvar, 3, 1.0, EPS, s_vvar)
            link(centre(vy[:], hv, vmv, 3))
            dve.wait_ge(s_idT, 1)
            dve.tensor_copy(id_col[:], bank[0].bitcast(BF16)[:, 0:2 * ROWS]).then_inc(s_idcol, 1)
            dve.wait_ge(s_idcol, 1)

            dve.wait_ge(loads["table"], 16)
            dve.tensor_reduce(tmax[:, 0:1], table_all[:, 0:512], AX.X, ALU.max)
            dve.wait_ge(s_vrs, 1)
            link(rescale(vy[:], vy[:], vrs, 3))
            row_stats(vy, vstat, vmv, vvar, 3, 1.0, EPS, s_vvar)
            link(centre(vy[:], vy[:], vmv, 3))
            link(dve.tensor_reduce(tmax[:, 1:2], table_all[:, 512:TABLE], AX.X, ALU.max))
            dve.wait_ge(s_vrs, 2)
            rescale(vy[:], vy[:], vrs, 3).then_inc(s_hl, 1)
            link(dve.tensor_reduce(nbmax[:], tmax[:], AX.X, ALU.max))
            dve.tensor_scalar(nbmax[:], nbmax[:], -1.0, None, ALU.mult).then_inc(s_nbmax, 1)
            dve.tensor_scalar(skip_j[:], id_col[:, ROWS:2 * ROWS], float(SKIP_ID), None, ALU.is_equal)
            def one_hot_rows():
                for c in range(BY_POOL, SEQS * JBLK):
                    col = c // JBLK * ROWS + c % JBLK
                    ins = dve.tensor_scalar(oneh_j[:, c, :], iota_h[:], id_col[:, col:col + 1], None, ALU.is_equal)
                ins.then_inc(s_onej, 1)

            def one_hot_cols(a, b):
                return dve.tensor_scalar(oneh_t[:, a:b], ids_all[:, a:b], iota_p[:, 0:1], None, ALU.is_equal)

            def late_one_hots():
                dve.wait_ge(loads["ids_all"], 16)
                link(dve.tensor_copy(ids_all[:, SEQS * LEN:], ids_all[:, LEN + FIRST:LEN + FIRST + 1]))
                link(dve.memset(ids_all[:, LEN + FIRST:LEN + FIRST + 1], float(SKIP_ID)))
                for s in range(SEQS):
                    one_hot_cols(LEN * s + FIRST, LEN * (s + 1) + s).then_inc(s_onet, 1)

            def early_one_hots():
                for s in range(SEQS):
                    one_hot_cols(LEN * s, LEN * s + FIRST)
                link(dve.tensor_tensor(gb_sum[:], vec[:, C_GB:C_GB + EXPERTS], vec[:, C_GB + EXPERTS:C_SC], ALU.add))

            def toeplitz():
                dve.wait_ge(s_expb, 1)
                link(dve.tensor_scalar(toe_hi[:, TOE_FLAT:TOE], hankel[:, ::-1], ESCALE, None, ALU.mult))
                link(dve.scalar_tensor_tensor(toe_lo[:, TOE_FLAT:TOE], hankel[:, ::-1], ESCALE, toe_hi[:, TOE_FLAT:TOE],
                                              ALU.mult, ALU.subtract))

            def toeplitz_flat():
                dve.tensor_copy(toe_hi[:, 0:TOE_FLAT], toe_hi[:, TOE_FLAT:TOE_FLAT + 1].to_broadcast([P, TOE_FLAT]))
                dve.tensor_copy(toe_lo[:, 0:TOE_FLAT], toe_lo[:, TOE_FLAT:TOE_FLAT + 1].to_broadcast([P, TOE_FLAT])).then_inc(s_toe, 1)

            def read_k():
                dve.wait_ge(s_qkv, 2)
                dve.tensor_copy(kT[:], bank[4][0:D, 0:IDS]).then_inc(s_ksb, 1)

            def read_counts():
                dve.wait_ge(s_cnt, 1)
                dve.tensor_copy(cnt[:].rearrange("p s c -> p (s c)"), bank[1][:, 0:4])
                dve.tensor_copy(skc[:], bank[1][:, 8:8 + ROWS]).then_inc(s_cntread, 1)
                dve.wait_ge(s_cntread, 1)
                dve.tensor_reduce(sk_half[:, 0:1], skc[:, NQ:ROWS], AX.X, ALU.add)
                dve.tensor_reduce(sk_half[:, 1:2], skc[:, 2 * NQ:ROWS], AX.X, ALU.add)
                dve.tensor_reduce(sk_half[:, 2:3], skc[:], AX.X, ALU.add)

            def penalties():
                dve.wait_ge(s_cntlate, SEQS)
                dve.tensor_copy(cnt_half[:, :, 1], cnt_late[:])
                link(dve.tensor_tensor(cnt_half[:, :, 0], cnt[:, :, 1], cnt_late[:], ALU.add))
                link(dve.tensor_tensor(cnt_half[:, :, 2], cnt[:, :, 0], cnt_half[:, :, 0], ALU.add))
                dve.tensor_scalar(absent[:, 0:2], cnt_half[:, :, 2], 0.0, ABSENT, ALU.is_equal, ALU.mult)
                link(dve.tensor_scalar(absent[:, 2:3], sk_half[:, 2:3], 0.0, ABSENT, ALU.is_equal, ALU.mult))
                dve.tensor_scalar(absent_d[:, 0:P], ident[:], absent[:, 0:1], None, ALU.mult)
                dve.tensor_scalar(absent_d[:, P:2 * P], ident[:], absent[:, 1:2], None, ALU.mult)
                dve.tensor_scalar(absent_d[:, 2 * P:2 * P + 1], ident[:, 0:1], absent[:, 2:3], None, ALU.mult).then_inc(s_absent, 1)

            def skip_columns():
                dve.tensor_scalar(skip_row[:], ids_all[0:1, LEN:], float(SKIP_ID), None, ALU.is_equal).then_inc(s_skrow, 1)

            def flat_weights():
                dve.wait_ge(s_toe, 1)
                link(dve.tensor_tensor(flat[:], toe_hi[:, 0:1], toe_lo[:, 0:1], ALU.add))
                dve.tensor_scalar(flat_w[:], cnt_half[:, :, 0:2], flat[:, 0:1], None, ALU.mult)
                dve.tensor_scalar(sk_flat[:], sk_half[:, 0:2], flat[:, 0:1], None, ALU.mult)

            def row_maxima():
                dve.wait_ge(s_g, 1)
                for n, (a, b) in enumerate(((S0, S1), (S1, SK), (SK, GW))):
                    ins = dve.tensor_reduce(gmax[:, n:n + 1], bank[6][:, a:b], AX.X, ALU.max)
                link(ins)
                dve.tensor_scalar(gmax[:], gmax[:], -1.0, None, ALU.mult).then_inc(s_gmax, 1)

            def values():
                dve.wait_ge(s_vproj, 1)
                dve.scalar_tensor_tensor(vp[:, :, 0:D], bank[2][:, 0:3 * D].rearrange("p (s d) -> p s d", d=D),
                                         vec[:, C_SC:C_SC + 1], bcast(vec[:, C_PB:C_PB + D], [P, 3, D], 1),
                                         ALU.mult, ALU.add).then_inc(s_vp, 1)
                dve.wait_ge(s_vp, 1)
                link(dve.tensor_reduce(vsum[:], vp[:, :, 0:D], AX.X, ALU.add))
                link(dve.tensor_scalar(vmean[:], vsum[:], 1.0 / D, None, ALU.mult))
                dve.tensor_tensor(vp[:, :, 0:D], vp[:, :, 0:D], vmean[:].unsqueeze(2).to_broadcast([P, 3, D]),
                                  ALU.subtract).then_inc(s_vp, 1)

            def split_exps():
                dve.wait_ge(s_eg, 3)
                link(dve.tensor_scalar(eg_hi[:], eg[:], ESCALE, None, ALU.mult))
                dve.scalar_tensor_tensor(eg_lo[:], eg[:], ESCALE, eg_hi[:], ALU.mult, ALU.subtract).then_inc(s_egs, 1)

            def bias_parts():
                dve.wait_ge(loads["b2"], 16)
                link(dve.tensor_scalar(b2_row[:], b2_row[:], YSCALE, None, ALU.mult))
                link(dve.tensor_copy(b2_part[:, 0], b2_row[:]))
                link(dve.tensor_tensor(b2_rest[:], b2_row[:], b2_part[:, 0], ALU.subtract))
                link(dve.tensor_copy(b2_part[:, 1], b2_rest[:]))
                link(dve.tensor_tensor(b2_rest[:], b2_rest[:], b2_part[:, 1], ALU.subtract))
                dve.tensor_copy(b2_part[:, 2], b2_rest[:]).then_inc(s_b2p, 1)

            def key_part(t):
                s, half = tile_s(t)
                dve.wait_ge(s_m, t + 1)
                dve.wait_ge(s_asb, t + 1)
                dve.scalar_tensor_tensor(pT[:, t, :], bank[M_BANK[t]][:, :], flat_w[:, s, half:half + 1],
                                         a_sb[:, t % 2, :], ALU.add, ALU.mult).then_inc(s_p, 1)

            def parts_of(g):
                m = SIZE[g]
                return (m, bank[3][:, 0:m * (D + 1)].rearrange("p (b d) -> p b d", d=D + 1),
                        bank[4][:, 0:m * D].rearrange("p (b d) -> p b d", d=D),
                        h_all[:, FIRST_BLOCK[g]:FIRST_BLOCK[g] + m, :])

            def rows_a(g):
                m = SIZE[g]
                dve.wait_ge(s_usq, g + 1)
                dve.tensor_scalar(deps[:, 0:m], usq[:, 0:m, D], EPS, None, ALU.mult)
                link(dve.tensor_reduce(uss[:, 0:m], usq[:, 0:m, 0:D], AX.X, ALU.add))
                dve.scalar_tensor_tensor(var1[:, 0:m], uss[:, 0:m], 1.0 / D, deps[:, 0:m], ALU.mult, ALU.add).then_inc(s_var1, 1)

            def rows_b(g):
                m, u, h, hg = parts_of(g)
                dve.wait_ge(s_rs1, g + 1)
                link(rescale(on[:, 0:m], u[:, :, 0:D], rs1[:, 0:m], m))
                link(dve.tensor_tensor(og[:, 0:m], on[:, 0:m], bcast(vec[:, C_G2:C_G2 + D], [P, m, D], 1), ALU.mult))
                dve.tensor_tensor(hg, og[:, 0:m], h, ALU.add).then_inc(s_h2, 1)

            def rows_b2(g):
                m, u, h, hg = parts_of(g)
                dve.wait_ge(s_h2, g + 1)
                row_stats(hg, stat, mv[:, 0:m], var2[:, 0:m], m, 1.0 / (XSCALE * XSCALE), EPS / (XSCALE * XSCALE), s_var2)
                link(centre(xc[:, 0:m], hg, mv[:, 0:m], m))

            def rows_c(g):
                m = SIZE[g]
                dve.wait_ge(s_rs2, g + 1)
                link(rescale(xn[:, 0:m], xc[:, 0:m], rs2[:, 0:m], m))
                if g >= 2:
                    dve.wait_ge(s_xT, g - 1)
                link(dve.tensor_copy(xs[:, g % 2, 0:m, 0, :], xn[:, 0:m]))
                dve.tensor_tensor(xs[:, g % 2, 0:m, 1, :], xn[:, 0:m], xs[:, g % 2, 0:m, 0, :], ALU.subtract).then_inc(s_xs, 1)

            def choose_a(g):
                m = SIZE[g]
                dve.wait_ge(s_lg, g + 1)
                dve.scalar_tensor_tensor(lg[:, 0:m], LOGITS[:, 0:m * EXPERTS].rearrange("p (b e) -> p b e", e=EXPERTS),
                                         1.0 / (XSCALE * XSCALE), bcast(gb_sum[:, :], [P, m, EXPERTS], 1),
                                         ALU.mult, ALU.add).then_inc(s_lgread, 1)
                dve.wait_ge(s_lgread, g + 1)
                for i in range(m):
                    ins = dve.max(top[:, i, :], lg[:, i, :])
                link(ins)
                dve.tensor_tensor(gd[:, 0:m], top[:, 0:m, 1], top[:, 0:m, 0], ALU.subtract).then_inc(s_gd, 1)
                for i in range(m):
                    ins = dve.max_index(tix[:, i, :], top[:, i, :], lg[:, i, :])
                link(ins)
                dve.tensor_copy(tixf[:, :, 0:m], tix[:, 0:m, 0:2].rearrange("p b j -> p j b"))

            def choose_b(g):
                m = SIZE[g]
                dve.wait_ge(s_ge, g + 1)
                link(dve.tensor_scalar(gs[:, 0:m], ge[:, 0:m], 1.0, YSCALE, ALU.add, ALU.mult))
                link(dve.reciprocal(gw[:, 0, 0:m], gs[:, 0:m]))
                dve.tensor_tensor(gw[:, 1, 0:m], gw[:, 0, 0:m], ge[:, 0:m], ALU.mult)
                four = [P, 2, m, EXPERTS]
                sm = sel[:, :, 0:m]
                link(dve.tensor_tensor(sm, iota_row[:, 0:EXPERTS].unsqueeze(1).unsqueeze(1).to_broadcast(four),
                                       tixf[:, :, 0:m].unsqueeze(3).to_broadcast(four), ALU.is_equal))
                link(dve.tensor_tensor(sm, sm, gw[:, :, 0:m].unsqueeze(3).to_broadcast(four), ALU.mult))
                link(dve.tensor_tensor(comb[:, g % 2, 0:m], sel[:, 0, 0:m], sel[:, 1, 0:m], ALU.add))

            def weigh(n):
                u, i = unit_of(n)
                dve.wait_ge(s_y, n + 1)
                dve.tensor_tensor(prod[:, n % 2], bank[Y_BANK[n % 2]][:, :].rearrange("p (e d) -> p e d", d=D),
                                  comb[:, u % 2, i, :].unsqueeze(2).to_broadcast([P, EXPERTS, D]),
                                  ALU.mult).then_inc(s_prod, 1)

            def gather(n):
                u, i = unit_of(n)
                dve.wait_ge(s_prod, n + 1)
                link(dve.tensor_reduce(acc[:, i, :], prod[:, n % 2].rearrange("p e d -> p d e"), AX.X, ALU.add))
                if i == SIZE[u] - 1:
                    bs = slice(FIRST_BLOCK[u], n + 1)
                    dve.tensor_tensor(fin_all[:, bs, :], acc[:, 0:SIZE[u]], h_all[:, bs, :], ALU.add).then_inc(s_fin, 1)

            def skip_key():
                dve.wait_ge(s_sk, 1)
                link(dve.tensor_copy(sk_a[:], bank[1][:, 8:16]))
                for half in range(2):
                    q = slice(NQ * half, NQ * half + NQ)
                    ins = dve.scalar_tensor_tensor(sk_p[:, q], bank[1][:, q], sk_flat[:, half:half + 1], sk_a[:, q],
                                                   ALU.add, ALU.mult)
                ins.then_inc(s_skp, 1)

            def skip_key_rows():
                dve.wait_ge(s_skT, 1)
                dve.tensor_copy(sk_pT[:], bank[1][0:8, 0:P]).then_inc(s_skTsb, 1)

            def low(k, e):
                n = EXPERTS * k + e
                dve.wait_ge(s_hid, n + 1)
                if k >= 2:
                    dve.wait_ge(s_y, FIRST_BLOCK[k - 1])
                link(dve.tensor_copy(hid_hi[:, k % 2, e, 0:P * SIZE[k]], hid[:, n % HSLOTS, 0:P * SIZE[k]]))
                low_part(dve, k, e).then_inc(s_lo_d, 1)

            one_hot_rows(); late_one_hots(); toeplitz(); toeplitz_flat(); read_k(); read_counts()
            penalties(); early_one_hots(); values(); flat_weights(); row_maxima(); skip_columns()
            bias_parts(); split_exps(); rows_a(0); rows_b(0); rows_b2(0); skip_key(); rows_c(0)
            key_part(0); skip_key_rows(); choose_a(0); choose_b(0); rows_a(1); rows_b(1); rows_b2(1)
            key_part(1); rows_c(1); rows_a(2); choose_a(1); rows_b(2); rows_b2(2); weigh(0); key_part(2)
            gather(0); rows_c(2); weigh(1); choose_b(1); rows_a(3); choose_a(2); gather(1); rows_b(3)
            rows_b2(3); weigh(2); gather(2); weigh(3); choose_b(2); gather(3); weigh(4); key_part(3)
            gather(4); weigh(5); rows_c(3); gather(5); rows_a(4); choose_a(3); weigh(6); gather(6)
            rows_b(4); rows_b2(4); weigh(7); gather(7); rows_c(4); weigh(8); gather(8); weigh(9)
            choose_b(3); choose_a(4); gather(9); weigh(10); gather(10); weigh(11); gather(11); weigh(12)
            gather(12); weigh(13); choose_b(4); low(4, 3); low(4, 5); gather(13); weigh(14); gather(14)
            weigh(15); gather(15); weigh(16); gather(16); weigh(17); gather(17)

        @block.tensor
        def _(pe_):
            mm = pe_.matmul

            pe_.wait_ge(s_ident, 1)
            pe_.wait_ge(s_ids, 1)
            for s in range(SEQS):
                ins = pe_.transpose(bank[0].bitcast(BF16)[:, ROWS * s:ROWS * s + ROWS], ids_b[:, s, :],
                                    ident_b[0:ROWS, 0:ROWS])
            ins.then_inc(s_idT, 1)
            pe_.wait_ge(s_hl, 1)
            pe_.wait_ge(s_ident, 2)
            for i in range(2):
                pe_.transpose(bank[2][0:D, P * i:P * i + P], vy[:, i, :], ident[:])
            pe_.transpose(bank[2][0:D, 2 * P:IDS], vy[0:1, 2, :], ident[0:1, 0:1]).then_inc(s_hT, 1)
            pe_.wait_ge(s_hTsb, 1)
            for i in range(3):
                mm(bank[3 + i][0:D, 0:IDS], qkv_sb[:, D * i:D * i + D], hvT[:], start=True, stop=True).then_inc(s_qkv, 1)
            pe_.wait_ge(s_onej, 1)
            pe_.wait_ge(s_onejp, BY_POOL)
            pe_.wait_ge(s_const, 2)
            for s in range(SEQS):
                for c in range(2):
                    for j in range(NQ):
                        mm(bank[1][:, 2 * s + c:2 * s + c + 1], oneh_j[:, JBLK * s + NQ * c + j, :], ones_h[:],
                           start=(j == 0), stop=(j == NQ - 1))
            mm(bank[1][:, 8:8 + ROWS], ones_b[:], skip_j[:], start=True, stop=True).then_inc(s_cnt, 1)

            def of_slot(x, i):
                return x[:, P * i:P * i + P] if i < 2 else x[:, 2 * P:IDS].to_broadcast([D, P])

            def project_values():
                pe_.wait_ge(s_qsb, 2)
                for i in range(3):
                    ins = mm(bank[2][:, D * i:D * i + D], of_slot(vT, i), qkv_sb[0:D, C_PROJ:C_PROJ + D], start=True, stop=True)
                ins.then_inc(s_vproj, 1)

            def weights(t, j0=0, j1=2 * NQ):
                s, half = tile_s(t)
                if t == 0 and j0 == 0:
                    pe_.wait_ge(s_toe, 1)
                if t == 1 and j0 == 0:
                    pe_.wait_ge(s_vp, 1)
                if t >= 2 and j0 == 0:
                    pe_.wait_ge(s_p, t)
                js = (NQ, 2 * NQ)[half]
                for j in range(j0, min(j1, js)):
                    z = TOE_FLAT + HALF * half - P * j
                    for part, toe in enumerate((toe_hi, toe_lo)):
                        ins = mm(bank[M_BANK[t]][:, :], oneh_j[:, JBLK * s + j, :], toe[:, z:z + HALF],
                                 start=(j == 0 and part == 0), stop=(j == js - 1 and part == 1))
                if j1 >= js:
                    ins.then_inc(s_m, 1)

            def scores(t):
                s, half = tile_s(t)
                if t == 0:
                    pe_.wait_ge(s_egs, 1)
                    pe_.wait_ge(s_skrow, 1)
                    pe_.wait_ge(s_qsb, 2)
                if t >= 1:
                    pe_.wait_ge(s_asb, t)
                    pe_.wait_ge(s_lgread, t)
                q0 = LEN * s + FIRST + HALF * half
                dst = bank[A_BANK[t]][:, :]
                mm(dst, eg_hi[:, P * s:P * s + P], oneh_t[:, q0:q0 + HALF], start=True, stop=False)
                ins = mm(dst, eg_lo[:, P * s:P * s + P], oneh_t[:, q0:q0 + HALF], start=False, stop=(s == 0))
                if s:
                    for part, e in enumerate((eg_hi, eg_lo)):
                        ins = mm(dst, e[0:1, SK:SK + P], skip_row[:, q0 - LEN:q0 - LEN + HALF], start=False, stop=part == 1)
                ins.then_inc(s_a, 1)

            def skip_weights(i0, i1):
                pe_.wait_ge(s_toe, 1)
                pe_.wait_ge(s_cntread, 1)
                for i in range(i0, i1):
                    js = NQ * (i // NQ + 1)
                    for j in range(js):
                        z = TOE_FLAT + P * (i - j)
                        for part, toe in enumerate((toe_hi, toe_lo)):
                            mm(bank[1][:, i:i + 1], toe[:, z:z + P], skip_j[:, j:j + 1],
                               start=(j == 0 and part == 0), stop=(j == js - 1 and part == 1))

            def skip_scores():
                pe_.wait_ge(s_egs, 1)
                pe_.wait_ge(s_skrow, 1)
                for i in range(2 * NQ):
                    q0 = FIRST + P * i
                    for part, e in enumerate((eg_hi, eg_lo)):
                        mm(bank[1][:, 8 + i:9 + i], oneh_t[:, LEN + q0:LEN + q0 + P], e[:, SK - 1:SK],
                           start=part == 0, stop=False)
                    for part, e in enumerate((eg_hi, eg_lo)):
                        ins = mm(bank[1][:, 8 + i:9 + i], skip_row[:, q0:q0 + P], e[0:1, GW - 1:GW],
                                 start=False, stop=part == 1)
                ins.then_inc(s_sk, 1)

            def skip_turn():
                pe_.wait_ge(s_skp, 1)
                pe_.transpose(bank[1][0:8, 0:P], sk_p[:], ident[:]).then_inc(s_skT, 1)

            def embedded(b, i):
                h = bank[4][:, D * i:D * (i + 1)]
                if b < 2:
                    for part in range(3):
                        mm(h, ident_h[:], h_part[:, part, 1 - b, :], start=part == 0, stop=part == 2)
                    return
                s, r = int(b < 10), (b - 2) % 8
                q0 = FIRST + P * r
                for part in range(3):
                    mm(h, oneh_t[:, LEN * s + q0:LEN * s + q0 + P], h_part[:, part, s, :],
                       start=part == 0, stop=(s == 0 and part == 2))
                if s:
                    for part in range(3):
                        mm(h, skip_row[:, q0:q0 + P], h_part[0:1, part, 2, :], start=False, stop=part == 2)

            def attended(b, i):
                u = bank[3][:, (D + 1) * i:(D + 1) * (i + 1)]
                if b < 2:
                    s = 1 - b
                    pe_.wait_ge(s_egTsb, 1)
                    pe_.wait_ge(s_vh, 1)
                    ins = mm(u, egT[:, s, :], vh[:, s, :], start=True, stop=(s == 0))
                    if s:
                        ins = mm(u, egT[0:1, 2, :], vh_skip[:], start=False, stop=True)
                    return ins
                s, r, t = int(b < 10), (b - 2) % 8, (b - 2) // NQ
                pe_.wait_ge(s_p, t + 1)
                ins = mm(u, pT[:, t, P * (r % NQ):P * (r % NQ) + P], vp[:, s, :], start=True, stop=(s == 0))
                if s:
                    pe_.wait_ge(s_skTsb, 1)
                    ins = mm(u, sk_pT[:], v_sel[:, r, :], start=False, stop=True)
                return ins

            def pair_scores():
                pe_.wait_ge(s_ksb, 1)
                pe_.wait_ge(s_absent, 1)
                for i, (a, b, k0) in enumerate(((S0, S1, 0), (S1, SK, P), (SK, GW, P))):
                    mm(bank[6][:, a:b], of_slot(qT, i), kT[:, k0:k0 + b - a], start=True, stop=False)
                    ins = mm(bank[6][:, a:b], ones_b[:], absent_d[:, k0:k0 + b - a], start=False, stop=True)
                ins.then_inc(s_g, 1)

            def turn_exps():
                pe_.wait_ge(s_eg, 3)
                for s in range(SEQS):
                    pe_.transpose(bank[3][:, P * s:P * s + P], eg[:, P * s:P * s + P], ident[:])
                pe_.transpose(bank[3][0:1, 2 * P:3 * P], eg[:, SK - 1:SK], ident[:]).then_inc(s_egT, 1)

            def embed(g):
                if g == 0:
                    pe_.wait_ge(s_hb, 1)
                    pe_.wait_ge(s_skrow, 1)
                    pe_.wait_ge(s_ksb, 1)
                else:
                    pe_.wait_ge(s_h2, g)
                for i in range(SIZE[g]):
                    embedded(FIRST_BLOCK[g] + i, i)

            def attend(b, n):
                g, i = unit_of(b)
                if g:
                    pe_.wait_ge(s_h2, g)
                for j in range(n):
                    ins = attended(b + j, i + j)
                if i + n == SIZE[g]:
                    ins.then_inc(s_u, 1)

            def turn(g):
                pe_.wait_ge(s_xs, g + 1)
                if g == 0:
                    pe_.wait_ge(s_asb, 1)
                else:
                    pe_.wait_ge(s_lgread, g)
                    if g < NQ:
                        pe_.wait_ge(s_asb, g + 1)
                for b in range(SIZE[g]):
                    ins = pe_.transpose(bank5h[:, P * b:P * b + P], xs[:, g % 2, b, :, :].rearrange("p a d -> p (a d)"),
                                        ident_h[:])
                ins.then_inc(s_xT, 1)

            def gate(g):
                pe_.wait_ge(s_xTsb, g + 1)
                for b in range(SIZE[g]):
                    for part, w in enumerate((w1_hi, w1_lo)):
                        ins = mm(LOGITS[:, EXPERTS * b:EXPERTS * (b + 1)], xT[:, g % 2, P * b:P * b + P],
                                 w[:, EXPERTS * HID:W1W], start=part == 0, stop=part == 1)
                ins.then_inc(s_lg, 1)

            def first_layer(k, e):
                n = EXPERTS * k + e
                if n == 0:
                    pe_.wait_ge(s_w1s, 1)
                m = P * SIZE[k]
                if e == 0:
                    pe_.wait_ge(s_xTsb, k + 1)
                if n < 2:
                    pe_.wait_ge(*((s_idcol, 1), (s_skTsb, 1))[n])
                else:
                    pe_.wait_ge(s_hid, n - 1)
                for part, w in enumerate((w1_hi, w1_lo)):
                    ins = mm(bank[n % 2][:, 0:m], w[:, HID * e:HID * (e + 1)], xT[:, k % 2, 0:m], start=part == 0, stop=part == 1)
                ins.then_inc(s_z, 1)

            def second_layer(n):
                k, i = unit_of(n)
                y = bank[Y_BANK[n % 2]]
                pe_.wait_ge(s_hid, EXPERTS * (k + 1))
                if n == 0:
                    pe_.wait_ge(loads["b2_k"], 16)
                    pe_.wait_ge(s_w2s, 1)
                    pe_.wait_ge(s_eg, 3)
                elif n == 1:
                    pe_.wait_ge(s_p, 1)
                else:
                    pe_.wait_ge(s_prod, n - 1)
                mm(y[:, :], ones_b[0:3, :], b2_k[:], start=True, stop=True)
                if i == 0 and LO_DVE[k]:
                    wait_lo(pe_, EXPERTS * k + LO_DVE[k][-1])
                for e in range(EXPERTS):
                    for w in (w2_hi, w2_lo):
                        mm(y[:, D * e:D * e + D], hid_hi[:, k % 2, e, P * i:P * i + P], w[:, D * e:D * e + D],
                           start=False, stop=False, skip_group_check=True)
                if i == 0:
                    wait_lo(pe_, EXPERTS * k + LO_POOL[k][-1])
                for e in range(EXPERTS):
                    ins = mm(y[:, D * e:D * e + D], hid_lo[:, k % 2, e, P * i:P * i + P], w2_hi[:, D * e:D * e + D],
                             start=False, stop=True, skip_group_check=True)
                ins.then_inc(s_y, 1)

            def look(dst, s, col, n, q):
                for part in range(3):
                    ins = mm(dst, oneh_t[:, col:col + n], fin_part[:, part, 1 - s, :], start=part == 0,
                             stop=(s == 0 and part == 2))
                if s:
                    for part in range(3):
                        ins = mm(dst, skip_row[:, q:q + n], fin_part[0:1, part, 2, :], start=False, stop=part == 2)
                return ins

            def look_up(n):
                if n == 0:
                    pe_.wait_ge(s_fpart, 1)
                    pe_.wait_ge(s_lgread, UNITS)
                else:
                    pe_.wait_ge(s_looked, n)
                if n < 2:
                    for i in range(FIRST // P):
                        ins = look(bank[5][:, D * i:D * i + D], n, LEN * n + P * i, P, P * i)
                else:
                    ins = look(bank[5][0:1, 0:D], 1, SEQS * LEN, 1, LEN)
                ins.then_inc(s_look, 1)

            project_values(); skip_weights(0, 4); pair_scores(); weights(0, 0, 4); turn_exps()
            weights(1, 0, 2); embed(0); weights(1, 2, 4); attend(0, 2); skip_weights(4, 8)
            skip_scores(); weights(1, 4, 6); scores(0); embed(1); skip_turn(); turn(0); gate(0)
            attend(2, 4); first_layer(0, 0); first_layer(0, 1); scores(1); first_layer(0, 2)
            first_layer(0, 3); weights(1, 6, 8); first_layer(0, 4); embed(2); first_layer(0, 5)
            attend(6, 4); first_layer(0, 6); turn(1); weights(2, 0, 2); gate(1); first_layer(0, 7)
            scores(2); first_layer(1, 0); first_layer(1, 1); second_layer(0); first_layer(1, 2)
            weights(2, 2, 4); first_layer(1, 3); second_layer(1); first_layer(1, 4); first_layer(1, 5)
            embed(3); attend(10, 4); first_layer(1, 6); turn(2); first_layer(1, 7); gate(2)
            weights(3, 0, 2); first_layer(2, 0); scores(3); weights(3, 2, 4); first_layer(2, 1)
            first_layer(2, 2); second_layer(2); second_layer(3); first_layer(2, 3); first_layer(2, 4)
            second_layer(4); first_layer(2, 5); weights(3, 4, 6); weights(3, 6, 8); first_layer(2, 6)
            second_layer(5); first_layer(2, 7); embed(4); attend(14, 4); turn(3); gate(3)
            first_layer(3, 0); first_layer(3, 1); second_layer(6); first_layer(3, 2); first_layer(3, 3)
            second_layer(7); first_layer(3, 4); first_layer(3, 5); second_layer(8); second_layer(9)
            first_layer(3, 6); turn(4); first_layer(3, 7); gate(4); first_layer(4, 0); first_layer(4, 1)
            second_layer(10); first_layer(4, 2); second_layer(11); second_layer(12); first_layer(4, 3)
            first_layer(4, 4); second_layer(13); first_layer(4, 5); first_layer(4, 6); look_up(0)
            first_layer(4, 7); second_layer(14); second_layer(15); second_layer(16); look_up(1)
            second_layer(17); look_up(2)


def kernel(**inputs):
    import numpy as _np
    import concourse.bacc as _bacc
    from concourse import mybir as _mybir
    from concourse.bass_utils import run_bass_kernel_spmd as _run

    a = {n.removeprefix("L0_"): _np.asarray(v) for n, v in inputs.items()}
    table = a["attn_bias_table"]
    w1 = a["ffn_W1"].transpose(1, 0, 2).reshape(D, -1)
    w1 = _np.concatenate([w1, a["ffn_Wg"]], 1)
    proj = _np.concatenate([a["attn_proj_w"], a["attn_ln1_g"][:, None], a["attn_ln1_b"][:, None]], 1)
    proj = _np.concatenate([proj, proj[:1]], 0)
    packed = {
        "x": a["x"],
        "token_w": a["tok_token_W"],
        "vecs": _np.concatenate([a["tok_pe"][0], a["tok_pe"][1], a["tok_token_W"][PAD_ID], a["attn_ln2_g"],
                                 a["attn_ln2_b"], a["attn_proj_b"], a["ffn_bg"], a["ffn_bias"],
                                 a["attn_scale"].reshape(1)]),
        "qkv": _np.concatenate([_np.concatenate([a["attn_qkv_w"], a["attn_qkv_b"][None]], 0), proj], 1),
        "bias_table": _np.concatenate([table, _np.repeat(table[-1:], 1151 - TABLE)]),
        "w1g": _np.concatenate([w1, w1], 0),
        "w2b1": _np.concatenate([a["ffn_W2"].transpose(1, 0, 2).reshape(HID, -1), a["ffn_b1"].T], 1),
        "b2": a["ffn_b2"].reshape(1, -1),
    }
    nc = _bacc.Bacc("TRN2", target_bir_lowering=False, num_devices=1)
    arrays, args = {}, []
    for name, v in packed.items():
        v = _np.ascontiguousarray(v)
        arrays[f"in_{name}_dram"] = v
        args.append(nc.dram_tensor(f"in_{name}_dram", v.shape, _mybir.dt.from_np(v.dtype), kind="ExternalInput").ap())
    args.append(nc.dram_tensor("out_0_dram", (SEQS, LEN, D), F32, kind="ExternalOutput").ap())
    build(nc, *args)
    r = _run(nc, [arrays], core_ids=[0])
    return r.results[0]["out_0_dram"]
```
